# Optimizing a Trainium2 kernel written in Bass

```python
import numpy as np
import jax
import jax.numpy as jnp

def _softmax(x, axis=-1):
    return jax.nn.softmax(x, axis=axis)

def _gelu(x):
    return jax.nn.gelu(x, approximate=True)

def _silu(x):
    return jax.nn.silu(x)

def _sigmoid(x):
    return jax.nn.sigmoid(x)

def _layernorm(x, axis=-1, eps=1e-05):
    m = jnp.mean(x, axis=axis, keepdims=True)
    v = jnp.var(x, axis=axis, keepdims=True)
    return (x - m) / jnp.sqrt(v + eps)

def _scatter_add(tgt, idx, src, axis=0):
    return tgt.at[idx].add(src)

def _segment_sum(src, seg, n):
    return jax.ops.segment_sum(src, seg, n)
kernel_name = 'mk_adaln_d1_jaxref_r8_e0be88'

def setup_inputs(seed: int=0):
    np.random.seed(seed)
    _w = jnp.asarray

    def _L0_attn_setup():
        import jax, jax.numpy as jnp
        import numpy as np
        D_MODEL = 128
        D_INNER = 2 * D_MODEL
        D_STATE = 16
        D_CONV = 4
        DT_RANK = D_MODEL // 16
        B, L = (2, 128)

        def _causal_depthwise_conv(u, conv_w, conv_b):
            K = conv_w.shape[-1]
            u = jnp.pad(u, ((0, 0), (0, 0), (K - 1, 0)))
            y = jax.lax.conv_general_dilated(u, conv_w, window_strides=(1,), padding='VALID', dimension_numbers=('NCH', 'OIH', 'NCH'), feature_group_count=u.shape[1])
            return y + conv_b[None, :, None]

        def _selective_scan(u, delta, A, Bm, Cm, D_skip):
            dA = jnp.exp(jnp.einsum('ble,en->blen', delta, A))
            dBu = jnp.einsum('ble,bln,ble->blen', delta, Bm, u)

            def step(h, inp):
                dA_t, dBu_t, C_t = inp
                h = dA_t * h + dBu_t
                y_t = jnp.einsum('ben,bn->be', h, C_t)
                return (h, y_t)
            h0 = jnp.zeros((u.shape[0], A.shape[0], A.shape[1]), dtype=u.dtype)
            xs = (jnp.swapaxes(dA, 0, 1), jnp.swapaxes(dBu, 0, 1), jnp.swapaxes(Cm, 0, 1))
            _, ys = jax.lax.scan(step, h0, xs)
            y = jnp.swapaxes(ys, 0, 1)
            return y + u * D_skip[None, None, :]
        key = jax.random.key(seed)
        ks = jax.random.split(key, 12)
        s = lambda fan_in: 1.0 / np.sqrt(fan_in)
        x = jax.random.normal(ks[0], (B, L, D_MODEL), dtype=jnp.float32)
        W_in = jax.random.normal(ks[1], (D_MODEL, 2 * D_INNER), dtype=jnp.float32) * s(D_MODEL)
        conv_w = jax.random.normal(ks[2], (D_INNER, 1, D_CONV), dtype=jnp.float32) * s(D_CONV)
        conv_b = jax.random.normal(ks[3], (D_INNER,), dtype=jnp.float32) * 0.02
        W_xp = jax.random.normal(ks[4], (D_INNER, DT_RANK + 2 * D_STATE), dtype=jnp.float32) * s(D_INNER)
        W_dt = jax.random.normal(ks[5], (DT_RANK, D_INNER), dtype=jnp.float32) * s(DT_RANK)
        dt = jnp.exp(jax.random.uniform(ks[6], (D_INNER,)) * (np.log(0.1) - np.log(0.001)) + np.log(0.001))
        dt_bias = dt + jnp.log(-jnp.expm1(-dt))
        A_log = jnp.log(jnp.broadcast_to(jnp.arange(1, D_STATE + 1, dtype=jnp.float32), (D_INNER, D_STATE)))
        D_skip = jnp.ones((D_INNER,), dtype=jnp.float32)
        W_out = jax.random.normal(ks[7], (D_INNER, D_MODEL), dtype=jnp.float32) * s(D_INNER)
        return {'x': x, 'W_in': W_in, 'conv_w': conv_w, 'conv_b': conv_b, 'W_xp': W_xp, 'W_dt': W_dt, 'dt_bias': dt_bias, 'A_log': A_log, 'D_skip': D_skip, 'W_out': W_out}
    _L0_attn_in = _L0_attn_setup()

    def _L0_ffn_setup():
        import jax, jax.numpy as jnp
        import numpy as np
        D_MODEL = 128
        DEPTH = 8
        M = 2 ** DEPTH
        N_INTERNAL = M - 1
        B, T = (8, 512)

        def _leaf_probs(gate):
            BT = gate.shape[0]
            lp = jnp.ones((BT, M), dtype=gate.dtype)
            for level in range(DEPTH):
                n = 2 ** level
                half = M // (2 * n)
                g = gate[:, n - 1:2 * n - 1]
                f = jnp.stack([1.0 - g, g], axis=-1)
                f = jnp.broadcast_to(f[..., None], (BT, n, 2, half))
                lp = lp * f.reshape(BT, M)
            return lp
        key = jax.random.key(seed)
        ks = jax.random.split(key, 7)
        x = jax.random.normal(ks[0], (B, T, D_MODEL), dtype=jnp.float32)
        Wq = jax.random.normal(ks[1], (D_MODEL, D_MODEL), dtype=jnp.float32) * 0.02
        routers = jax.random.normal(ks[2], (N_INTERNAL, D_MODEL), dtype=jnp.float32) * 0.02
        leaf_keys = jax.random.normal(ks[3], (M, D_MODEL), dtype=jnp.float32) * 0.02
        leaf_values = jax.random.normal(ks[4], (M, D_MODEL), dtype=jnp.float32) * 0.02
        Wout_w = jax.random.normal(ks[5], (D_MODEL, D_MODEL), dtype=jnp.float32) * 0.02
        Wout_b = jax.random.normal(ks[6], (D_MODEL,), dtype=jnp.float32) * 0.02
        return {'x': x, 'Wq': Wq, 'routers': routers, 'leaf_keys': leaf_keys, 'leaf_values': leaf_values, 'Wout_w': Wout_w, 'Wout_b': Wout_b}
    _L0_ffn_in = _L0_ffn_setup()
    _L0_c = _w((lambda *s: np.random.randn(*s).astype(np.float32) * 0.05)(2, 128))
    _L0_wmod = _w((lambda *s: np.random.randn(*s).astype(np.float32) * 0.05)(128, 6 * 128) * 128 ** (-0.5))
    _d = {'L0_attn_x': _L0_attn_in['x'], 'L0_attn_W_in': _L0_attn_in['W_in'], 'L0_attn_conv_w': _L0_attn_in['conv_w'], 'L0_attn_conv_b': _L0_attn_in['conv_b'], 'L0_attn_W_xp': _L0_attn_in['W_xp'], 'L0_attn_W_dt': _L0_attn_in['W_dt'], 'L0_attn_dt_bias': _L0_attn_in['dt_bias'], 'L0_attn_A_log': _L0_attn_in['A_log'], 'L0_attn_D_skip': _L0_attn_in['D_skip'], 'L0_attn_W_out': _L0_attn_in['W_out'], 'L0_ffn_Wq': _L0_ffn_in['Wq'], 'L0_ffn_routers': _L0_ffn_in['routers'], 'L0_ffn_leaf_keys': _L0_ffn_in['leaf_keys'], 'L0_ffn_leaf_values': _L0_ffn_in['leaf_values'], 'L0_ffn_Wout_w': _L0_ffn_in['Wout_w'], 'L0_ffn_Wout_b': _L0_ffn_in['Wout_b'], 'L0_c': _L0_c, 'L0_wmod': _L0_wmod}
    _x0 = _d['L0_attn_x']
    _d['L0_attn_x'] = jax.random.normal(jax.random.fold_in(jax.random.key(seed), 1), (2, 2048, 128), dtype=_x0.dtype)
    del _x0
    return _d

def reference(L0_attn_x, L0_attn_W_in, L0_attn_conv_w, L0_attn_conv_b, L0_attn_W_xp, L0_attn_W_dt, L0_attn_dt_bias, L0_attn_A_log, L0_attn_D_skip, L0_attn_W_out, L0_ffn_Wq, L0_ffn_routers, L0_ffn_leaf_keys, L0_ffn_leaf_values, L0_ffn_Wout_w, L0_ffn_Wout_b, L0_c, L0_wmod):

    def _L0_attn_ref(x, W_in, conv_w, conv_b, W_xp, W_dt, dt_bias, A_log, D_skip, W_out):
        import jax, jax.numpy as jnp
        import numpy as np
        D_MODEL = 128
        D_INNER = 2 * D_MODEL
        D_STATE = 16
        D_CONV = 4
        DT_RANK = D_MODEL // 16
        B, L = (2, 128)

        def _causal_depthwise_conv(u, conv_w, conv_b):
            K = conv_w.shape[-1]
            u = jnp.pad(u, ((0, 0), (0, 0), (K - 1, 0)))
            y = jax.lax.conv_general_dilated(u, conv_w, window_strides=(1,), padding='VALID', dimension_numbers=('NCH', 'OIH', 'NCH'), feature_group_count=u.shape[1])
            return y + conv_b[None, :, None]

        def _selective_scan(u, delta, A, Bm, Cm, D_skip):
            dA = jnp.exp(jnp.einsum('ble,en->blen', delta, A))
            dBu = jnp.einsum('ble,bln,ble->blen', delta, Bm, u)

            def step(h, inp):
                dA_t, dBu_t, C_t = inp
                h = dA_t * h + dBu_t
                y_t = jnp.einsum('ben,bn->be', h, C_t)
                return (h, y_t)
            h0 = jnp.zeros((u.shape[0], A.shape[0], A.shape[1]), dtype=u.dtype)
            xs = (jnp.swapaxes(dA, 0, 1), jnp.swapaxes(dBu, 0, 1), jnp.swapaxes(Cm, 0, 1))
            _, ys = jax.lax.scan(step, h0, xs)
            y = jnp.swapaxes(ys, 0, 1)
            return y + u * D_skip[None, None, :]
        xz = x @ W_in
        xp, z = jnp.split(xz, 2, axis=-1)
        u = _causal_depthwise_conv(jnp.swapaxes(xp, 1, 2), conv_w, conv_b)
        u = jax.nn.silu(jnp.swapaxes(u, 1, 2))
        x_dbl = u @ W_xp
        dt_r, Bm, Cm = jnp.split(x_dbl, [DT_RANK, DT_RANK + D_STATE], axis=-1)
        delta = jax.nn.softplus(dt_r @ W_dt + dt_bias)
        A = -jnp.exp(A_log)
        y = _selective_scan(u, delta, A, Bm, Cm, D_skip)
        y = y * jax.nn.silu(z)
        return y @ W_out

    def _L0_ffn_ref(x, Wq, routers, leaf_keys, leaf_values, Wout_w, Wout_b):
        import jax, jax.numpy as jnp
        import numpy as np
        D_MODEL = 128
        DEPTH = 8
        M = 2 ** DEPTH
        N_INTERNAL = M - 1
        B, T = (8, 512)

        def _leaf_probs(gate):
            BT = gate.shape[0]
            lp = jnp.ones((BT, M), dtype=gate.dtype)
            for level in range(DEPTH):
                n = 2 ** level
                half = M // (2 * n)
                g = gate[:, n - 1:2 * n - 1]
                f = jnp.stack([1.0 - g, g], axis=-1)
                f = jnp.broadcast_to(f[..., None], (BT, n, 2, half))
                lp = lp * f.reshape(BT, M)
            return lp
        Bv, Tv, d = x.shape
        q = jnp.einsum('btd,ed->bte', x, Wq)
        q_flat = q.reshape(Bv * Tv, d)
        gate = jax.nn.sigmoid(q_flat @ routers.T)
        leaf_prob = _leaf_probs(gate)
        ret = (leaf_prob @ leaf_values).reshape(Bv, Tv, d)
        return jnp.einsum('btd,ed->bte', ret, Wout_w) + Wout_b
    x = L0_attn_x
    mod = (_silu(L0_c) @ L0_wmod).reshape(L0_c.shape[0], 6, 1, -1)
    sa, ca, ga, sb, cb, gb = (mod[:, 0], mod[:, 1], mod[:, 2], mod[:, 3], mod[:, 4], mod[:, 5])
    ga = (2 * (ga >= 0) - 1) * jnp.maximum(jnp.abs(ga), 0.25)
    gb = (2 * (gb >= 0) - 1) * jnp.maximum(jnp.abs(gb), 0.25)
    h = _layernorm(x, axis=-1) * (1 + ca) + sa
    x = x + ga * _L0_attn_ref(h, L0_attn_W_in, L0_attn_conv_w, L0_attn_conv_b, L0_attn_W_xp, L0_attn_W_dt, L0_attn_dt_bias, L0_attn_A_log, L0_attn_D_skip, L0_attn_W_out)
    h = _layernorm(x, axis=-1) * (1 + cb) + sb
    x = x + gb * _L0_ffn_ref(h, L0_ffn_Wq, L0_ffn_routers, L0_ffn_leaf_keys, L0_ffn_leaf_values, L0_ffn_Wout_w, L0_ffn_Wout_b)
    return x

_drawn_inputs = setup_inputs


def setup_inputs(seed=0):
    import zlib

    import numpy as np

    out = dict(_drawn_inputs(seed))
    spreads = {'L0_attn_D_skip': (1.0, 0.6)}
    factors = {'L0_attn_conv_b': 8.0,
     'L0_attn_W_xp': 3.651,
     'L0_attn_W_dt': 7.571,
     'L0_attn_dt_bias': 6.864,
     'L0_attn_A_log': 7.46,
     'L0_ffn_Wq': 64.0,
     'L0_ffn_routers': 64.0,
     'L0_ffn_leaf_values': 64.0,
     'L0_ffn_Wout_w': 64.0,
     'L0_ffn_Wout_b': 64.0}
    for name, (base, spread) in spreads.items():
        noise = np.random.default_rng([zlib.crc32(name.encode()), seed]).standard_normal(out[name].shape)
        drawn = base * np.exp(spread * noise) if base else spread * noise
        out[name] = jnp.asarray(drawn.astype(out[name].dtype))
    for name, factor in factors.items():
        out[name] = (out[name] * factor).astype(out[name].dtype)
    return out
```

```python
import math

import concourse.bass as bass
from concourse import mybir
from contextlib import ExitStack


def bass_adaln_mamba_tree_ffn_kernel(
    nc: bass.Bass,
    x: bass.AP,
    W_in: bass.AP,
    conv_w: bass.AP,
    conv_b: bass.AP,
    W_xp: bass.AP,
    W_dt: bass.AP,
    dt_bias: bass.AP,
    A_log: bass.AP,
    D_skip: bass.AP,
    W_out: bass.AP,
    Wq: bass.AP,
    routers: bass.AP,
    leaf_values: bass.AP,
    Wo: bass.AP,
    Wo_b: bass.AP,
    c: bass.AP,
    wmod: bass.AP,
    out: bass.AP,
):
    f32 = mybir.dt.float32
    bf16 = mybir.dt.bfloat16
    ALU = mybir.AluOpType
    ACT = mybir.ActivationFunctionType

    P = 128
    BATCH, L, DM = x.shape
    DI = W_out.shape[0]
    HALVES = DI // P
    R = W_dt.shape[0]
    N = (W_xp.shape[1] - R) // 2
    TAPS = conv_w.shape[2]
    HALO = TAPS - 1
    T = 512
    TILES = T // P
    CHUNKS = L // T
    GROUPS = BATCH * CHUNKS
    STEPS = N * HALVES
    K = GROUPS * STEPS
    NODES = routers.shape[0]
    LEAVES = leaf_values.shape[0]
    DEPTH = LEAVES.bit_length() - 1
    EPS = 1e-5
    THETA = 2.0 ** -5
    KNEE = -math.log(THETA)
    GATE_MIN = 0.25
    QUARTERS = 4
    NQ = N // QUARTERS
    B_HI, C_ROW, DT_ROW, B_MID, B_LO = 0, N, 2 * N, 64, 96
    ONE_ROW = DT_ROW + R

    RB, RY, RD, RH, RM = 3, 3, 4, 4, 2
    AHEAD_EXP, AHEAD_FILL, AHEAD_DBU, LAG_SUM = 3, 2, 1, 3

    F_STATS, F_XHAT, F_TR, F_XP, F_CONV, F_Z = 0, 2, 3, (5, 6), (8, 10), (9, 10)
    F_SILU, F_XD, F_HI, F_R1, F_MID, F_R2, F_LO = 15, 17, 18, 19, 20, 21, 22
    F_DT, F_SP, F_POLY, F_DELTA, F_DU = (19, 20), 21, (23, 24), 25, (25, 26)
    T_GATE, T_OUT, T_ADD, T_STATS, T_XHAT, T_TR = (4, 5), 7, 8, 9, 10, 12
    T_NODE, T_TANH, T_SIG, T_LEAF, T_PT, T_FF, T_FIN = (13, 14), 15, 16, (18, 20, 22, 24), (27, 28), 30, 31

    JOBS = [("f", "tr", 0, F_TR), ("f", "xp", 0, F_XP[0]), ("f", "xp", 1, F_XP[1]), ("t", "out", 0, T_OUT),
            ("f", "z", 0, F_Z[0]), ("f", "z", 1, F_Z[1]), ("t", "tr", 0, T_TR), ("t", "node", 0, T_NODE[0]),
            ("t", "node", 1, T_NODE[1]), ("f", "xd", 0, F_XD), ("f", "dt", 0, F_DT[0]), ("f", "dt", 1, F_DT[1]),
            ("t", "pt", 0, T_PT[0]), ("t", "pt", 1, T_PT[1]), ("t", "ff", 0, T_FF)]
    BY_DVE = {"out", "dt", "ff"}
    job_at, freed_at, freed = {}, [], {"act": 0, "dve": 0}
    for g in range(-1, GROUPS + 1):
        for side, name, part, _ in JOBS:
            own = g + 1 if side == "f" else g - 1
            if 0 <= own < GROUPS:
                job_at[side, name, part, own] = len(freed_at)
                by = "dve" if name in BY_DVE else "act"
                freed[by] += 1
                freed_at.append((by, freed[by]))

    ctx = ExitStack()
    with ctx:
        def sb(name, shape, dt=f32):
            return ctx.enter_context(nc.sbuf_tensor(name, shape, dt))

        def sem(name):
            return ctx.enter_context(nc.semaphore(name))

        ident = sb("ident", [P, P])
        sel = sb("sel", [P, N, P], bf16)
        ones = sb("ones", [P, P])
        half_col = sb("half_col", [P, 1])
        third_col = sb("third_col", [P, 1])
        knee_col = sb("knee_col", [P, 1])
        neg_knee_col = sb("neg_knee_col", [P, 1])
        knee_ln = sb("knee_ln", [P, 1])
        one_at = sb("one_at", [P, 1])
        w_in = sb("w_in", [P, 2 * DI])
        w_xp = sb("w_xp", [P, HALVES, P])
        w_dt = sb("w_dt", [P, DI])
        w_out = sb("w_out", [P, HALVES, DM])
        wq = sb("wq", [P, DM])
        rout = sb("rout", [P, 2, DM])
        leafv = sb("leafv", [P, 2, DM])
        wo = sb("wo", [P, DM])
        wo_b = sb("wo_b", [1, DM])
        taps = sb("taps", [P, HALVES, TAPS])
        cbias = sb("cbias", [P, HALVES])
        dskip = sb("dskip", [P, HALVES])
        alog = sb("alog", [P, HALVES, N])
        a_neg = sb("a_neg", [P, HALVES, N])
        c_col = sb("c_col", [P, BATCH])
        c_silu = sb("c_silu", [P, BATCH])
        c_wide = sb("c_wide", [P, BATCH, P])
        w_mod = sb("w_mod", [P, 6, DM])
        mod_col = sb("mod_col", [P, 6, BATCH])
        gate_raw = sb("gate_raw", [P, BATCH, 2, DM])
        gate_sgn = sb("gate_sgn", [P, BATCH, 2, DM])
        gate_abs = sb("gate_abs", [P, BATCH, 2, DM])
        rout_t = sb("rout_t", [P, 2 * P])
        leafv_t = sb("leafv_t", [P, 2 * P])
        wo_t = sb("wo_t", [P, DM])
        w_node = sb("w_node", [P, 2 * P])
        leaf_out = sb("leaf_out", [P, 2, DM])
        w_out_g = sb("w_out_g", [P, BATCH, HALVES, DM])
        leaf_out_g = sb("leaf_out_g", [P, BATCH, 2, DM])
        wo_b_g = sb("wo_b_g", [1, BATCH, DM])
        diag_d = sb("diag_d", [P, HALVES, P])
        xs = sb("xs", [P, GROUPS * TILES, DM])
        dA = sb("dA", [P, RD, T])
        h = sb("h", [P, RH, T])
        hc = sb("hc", [P, RH, T])
        state = sb("state", [P, STEPS])
        c_rows = sb("c_rows", [P, QUARTERS, NQ, T])
        zu = sb("zu", [P, 2, 2 * HALVES, T])
        delta = sb("delta", [P, 2, HALVES, T])
        du = sb("du", [P, 2, HALVES, T])
        b_parts = sb("b_parts", [P, 2, T], bf16)
        f_bn = sb("f_bn", [P, TILES, 6])
        f_mv = sb("f_mv", [P, TILES, 2])
        f_ve = sb("f_ve", [P, TILES])
        f_rs = sb("f_rs", [P, TILES])
        f_xhat = sb("f_xhat", [P, TILES, DM])
        f_hT = sb("f_hT", [P, T])
        xpad = sb("xpad", [P, HALVES, HALO + T])
        xd = sb("xd", [P, T])
        b_rest = sb("b_rest", [P, T])
        sp_abs = sb("sp_abs", [P, HALVES, T])
        sp_e = sb("sp_e", [P, HALVES, T])
        sp_t = sb("sp_t", [P, HALVES, T])
        sp_ln = sb("sp_ln", [P, HALVES, T])
        yg = sb("yg", [P, HALVES, T])
        t_bn = sb("t_bn", [P, TILES, 6])
        t_mv = sb("t_mv", [P, TILES, 2])
        t_ve = sb("t_ve", [P, TILES])
        t_rs = sb("t_rs", [P, TILES])
        t_xhat = sb("t_xhat", [P, TILES, DM])
        t_hT = sb("t_hT", [P, T])
        th = sb("th", [P, TILES, LEAVES])
        go_r = sb("go_r", [P, TILES, LEAVES])
        go_l = sb("go_l", [P, TILES, LEAVES])
        prob = [sb(f"prob{i}", [P, TILES, LEAVES]) for i in range(2)]
        probT = sb("probT", [P, 2, T])

        bb = [ctx.enter_context(nc.psum_tensor(f"bb{i}", [P, T], f32)) for i in range(RB)]
        yb = [ctx.enter_context(nc.psum_tensor(f"yb{i}", [P, T], f32)) for i in range(RY)]
        mb = [ctx.enter_context(nc.psum_tensor(f"mb{i}", [P, T], f32)) for i in range(RM)]
        c_dram = nc.dram_tensor("c_dram", [GROUPS, N, T], f32, kind="Internal").ap()

        s_w = sem("weights_loaded")
        s_x = sem("x_loaded")
        s_rt = sem("rout_zeroed")
        s_wz = sem("w_xp_zeroed")
        s_const = sem("constants_made")
        s_pool = sem("pool_seq")
        s_dseq = sem("dve_seq")
        s_aseq = sem("act_seq")
        s_pre_pe = sem("pre_products")
        s_pre_cp = sem("pre_copied")
        s_csilu = sem("c_silu_ready")
        s_cwide = sem("c_wide_ready")
        s_aexp = sem("a_exp_ready")
        s_aneg = sem("a_neg_ready")
        s_wready = sem("scaled_weights_ready")
        s_fill = sem("b_filled")
        s_dbu = sem("dbu_done")
        s_dA = sem("dA_done")
        s_scan = sem("scan_done")
        s_save = sem("state_saved")
        s_hc = sem("hc_done")
        s_sum = sem("sum_done")
        s_job = sem("job_done")
        s_free = {"act": sem("job_read_by_act"), "dve": sem("job_read_by_dve")}
        s_fvar = sem("f_var_ready")
        s_frs = sem("f_rstd_ready")
        s_fxh = sem("f_xhat_ready")
        s_fhT = sem("f_hT_ready")
        s_xpad = sem("xp_copied")
        s_conv = sem("conv_done")
        s_silu = sem("silu_done")
        s_xd = sem("xd_ready")
        s_hi = sem("b_hi_ready")
        s_r1 = sem("b_rest1_ready")
        s_mid = sem("b_mid_ready")
        s_r2 = sem("b_rest2_ready")
        s_lo = sem("b_parts_ready")
        s_poly = sem("softplus_series_ready")
        s_sp = sem("softplus_ln_ready")
        s_delta = sem("delta_ready")
        s_du = sem("du_ready")
        s_cst = sem("c_stored")
        s_cld = [sem(f"c_loaded{q}") for q in range(QUARTERS)]
        s_gate = sem("y_gated")
        s_add = sem("mamba_added")
        s_tvar = sem("t_var_ready")
        s_trs = sem("t_rstd_ready")
        s_txh = sem("t_xhat_ready")
        s_thT = sem("t_hT_ready")
        s_sig = sem("node_sigmoids_ready")
        s_prob = sem("leaf_probs_ready")
        s_pT = sem("probT_ready")
        s_fin = sem("out_ready")
        s_out = sem("out_stored")

        block = ctx.enter_context(nc.Block())

        def job(side, name, part, g):
            n = job_at[side, name, part, g]
            return n, mb[n % RM]

        def wait_job(eng, n):
            eng.wait_ge(s_job, n + 1)

        def wait_bank(eng, n):
            if n >= RM:
                by, count = freed_at[n - RM]
                eng.wait_ge(s_free[by], count)

        def saves(k):
            g, s = divmod(k, STEPS)
            per_batch = (CHUNKS - 1) * STEPS
            return (g // CHUNKS) * per_batch + (g % CHUNKS) * STEPS + (s if g % CHUNKS < CHUNKS - 1 else 0)

        n_weights = 0

        @block.sync
        def _(sp):
            nonlocal n_weights

            def load(dst, src):
                nonlocal n_weights
                n_weights += 1
                sp.dma_start(dst, src, allow_slow_non_contiguous=True).then_inc(s_w, 16)

            def load_x(g):
                b, ch = divmod(g, CHUNKS)
                sp.dma_start(xs[:, g * TILES:(g + 1) * TILES, :],
                             x[b, ch * T:(ch + 1) * T, :].rearrange("(i p) d -> p i d", p=P)).then_inc(s_x, 16)

            load_x(0)
            load(c_col[:, :], c.rearrange("b k -> k b"))
            load(w_mod[:, :, :], wmod.rearrange("k (j d) -> k j d", j=6))
            load(w_in[:, :], W_in)
            load(taps[:, :, :], conv_w.rearrange("(h p) o k -> p h (o k)", p=P))
            load(cbias[:, :], conv_b.rearrange("(h p) -> p h", p=P))
            load(dskip[:, :], D_skip.rearrange("(h p) -> p h", p=P))
            load(alog[:, :, :], A_log.rearrange("(h p) n -> p h n", p=P))
            load(w_dt[DT_ROW:DT_ROW + R, :], W_dt)
            load(w_dt[ONE_ROW:ONE_ROW + 1, :], dt_bias.rearrange("(a n) -> a n", a=1))
            load(w_out[:, :, :], W_out.rearrange("(h p) d -> p h d", p=P))
            load(wq[:, :], Wq)
            load(leafv[:, :, :], leaf_values.rearrange("(h p) d -> p h d", p=P))
            load(wo[:, :], Wo)
            load(wo_b[:, :], Wo_b.rearrange("(a n) -> a n", a=1))
            sp.wait_ge(s_wz, 1)
            xp_v = W_xp.rearrange("(h p) j -> p h j", p=P)
            for row, first, count in ((B_HI, R, N), (C_ROW, R + N, N), (DT_ROW, 0, R), (B_MID, R, N), (B_LO, R, N)):
                load(w_xp[:, :, row:row + count], xp_v[:, :, first:first + count])
            sp.wait_ge(s_rt, 1)
            load(rout[:, 0, :], routers[0:P, :])
            load(rout[0:NODES - P, 1, :], routers[P:NODES, :])
            for g in range(1, GROUPS):
                load_x(g)

            for g in range(-1, GROUPS + 1):
                f, t = g + 1, g - 1
                if f < GROUPS:
                    sp.wait_ge(s_xd, f + 1)
                    sp.dma_start(c_dram[f, :, :], xd[C_ROW:C_ROW + N, :]).then_inc(s_cst, 16)
                    sp.wait_ge(s_cst, 16 * (f + 1))
                    for q in range(QUARTERS):
                        if g >= 0:
                            sp.wait_ge(s_hc, g * STEPS + (q + 1) * NQ * HALVES)
                        src = c_dram[f, q * NQ:(q + 1) * NQ, :].rearrange("n t -> (n t)")
                        sp.dma_start(c_rows[:, q, :, :].rearrange("p n t -> p (n t)"),
                                     src.partition_broadcast(P)).then_inc(s_cld[q], 16)
                if t >= 0:
                    b, ch = divmod(t, CHUNKS)
                    sp.wait_ge(s_fin, t + 1)
                    sp.dma_start(out[b, ch * T:(ch + 1) * T, :].rearrange("(i p) d -> p i d", p=P),
                                 xs[:, t * TILES:(t + 1) * TILES, :]).then_inc(s_out, 16)
            sp.wait_ge(s_out, 16 * GROUPS)

        @block.gpsimd
        def _(pool):
            seq = 0

            def chain(ins):
                nonlocal seq
                seq += 1
                ins.then_inc(s_pool, 1)
                pool.wait_ge(s_pool, seq)

            nc.gpsimd.memset(w_xp[:, :, :], 0.0).then_inc(s_wz, 1)
            nc.gpsimd.memset(rout[:, 1, :], 0.0).then_inc(s_rt, 1)
            chain(nc.gpsimd.memset(ident[:, :], 0.0))
            chain(nc.gpsimd.affine_select(out=ident[:, :], in_=ident[:, :], compare_op=ALU.not_equal, fill=1.0,
                                          base=0, pattern=[[-1, P]], channel_multiplier=1))
            chain(nc.gpsimd.memset(one_at[:, :], 0.0))
            chain(nc.gpsimd.affine_select(out=one_at[:, :], in_=one_at[:, :], compare_op=ALU.not_equal, fill=1.0,
                                          base=-ONE_ROW, pattern=[[0, 1]], channel_multiplier=1))
            nc.gpsimd.memset(half_col[:, :], 0.5)
            nc.gpsimd.memset(third_col[:, :], 1.0 / 3.0)
            nc.gpsimd.memset(knee_col[:, :], KNEE)
            nc.gpsimd.memset(neg_knee_col[:, :], -KNEE)
            chain(nc.gpsimd.memset(ones[:, :], 1.0))
            nc.gpsimd.memset(xpad[:, :, 0:HALO], 0.0).then_inc(s_const, 1)
            chain(nc.gpsimd.memset(sel[:, :, :], 0.0))
            for first in (B_HI, B_MID, B_LO):
                chain(nc.gpsimd.affine_select(out=sel[:, :, :], in_=sel[:, :, :], compare_op=ALU.not_equal,
                                              fill=1.0, base=-first, pattern=[[-1, N], [0, P]],
                                              channel_multiplier=1))
            nc.gpsimd.memset(half_col[:, :], 0.5).then_inc(s_const, 1)

            def leaf_level(level):
                n = 1 << level
                dst = prob[level % 2][:, :, 0:2 * n].rearrange("p i (n two) -> p i n two", two=2)
                src = prob[(level + 1) % 2][:, :, 0:n]
                for side, go in ((0, go_l), (1, go_r)):
                    node = go[:, :, n - 1:2 * n - 1]
                    if level == 0:
                        last = nc.gpsimd.tensor_copy(dst[:, :, :, side], node)
                    else:
                        last = nc.gpsimd.tensor_tensor(dst[:, :, :, side], src, node, ALU.mult)
                    if side == 0:
                        last.then_inc(s_pool, 1)
                return last

            for g in range(-1, GROUPS + 1):
                f, t = g + 1, g - 1
                front, tail = f < GROUPS, t >= 0
                for s in range(STEPS):
                    if 0 <= g < GROUPS:
                        k, n = g * STEPS + s, s // HALVES
                        q = n // NQ
                        if s % (NQ * HALVES) == 0:
                            pool.wait_ge(s_cld[q], 16 * (g + 1))
                        pool.wait_ge(s_scan, k + 1)
                        if k >= RH:
                            pool.wait_ge(s_sum, k - RH + 1)
                        nc.gpsimd.tensor_tensor(hc[:, k % RH, :], h[:, k % RH, :], c_rows[:, q, n % NQ, :],
                                                ALU.mult).then_inc(s_hc, 1)
                    if front and s == F_R1:
                        pool.wait_ge(s_hi, f + 1)
                        nc.gpsimd.tensor_tensor(b_rest[:, :], xd[:, :], b_parts[:, f % 2, :],
                                                ALU.subtract).then_inc(s_r1, 1)
                    if front and s == F_R2:
                        pool.wait_ge(s_r1, f + 1)
                        pool.wait_ge(s_mid, f + 1)
                        nc.gpsimd.tensor_tensor(b_rest[:, :], b_rest[:, :], b_parts[:, f % 2, :],
                                                ALU.subtract).then_inc(s_r2, 1)
                    if front and s in F_DU:
                        half = F_DU.index(s)
                        pool.wait_ge(s_delta, HALVES * f + half + 1)
                        pool.wait_ge(s_silu, f + 1)
                        nc.gpsimd.tensor_tensor(du[:, f % 2, half, :], delta[:, f % 2, half, :],
                                                zu[:, f % 2, HALVES + half, :], ALU.mult).then_inc(s_du, 1)
                    if tail and s in T_LEAF:
                        if s == T_LEAF[0]:
                            pool.wait_ge(s_sig, t + 1)
                            levels = range(0, DEPTH - 3)
                        else:
                            levels = [DEPTH - 4 + T_LEAF.index(s)]
                        for level in levels:
                            if level:
                                pool.wait_ge(s_pool, seq)
                            if level == DEPTH - 1 and t >= 1:
                                wait_job(pool, job("t", "pt", 1, t - 1)[0])
                            last = leaf_level(level)
                            seq += 1
                            if level == DEPTH - 1:
                                last.then_inc(s_prob, 1)
                            else:
                                seq += 1
                                last.then_inc(s_pool, 1)

        @block.scalar
        def _(act):
            seq = 0

            def chain(ins):
                nonlocal seq
                seq += 1
                ins.then_inc(s_aseq, 1)
                act.wait_ge(s_aseq, seq)

            def rstd(var, out_, done, done_sem):
                act.wait_ge(var, done)
                chain(nc.scalar.activation(out_[0][:, :], out_[1][:, :], ACT.Ln))
                nc.scalar.activation(out_[0][:, :], out_[0][:, :], ACT.Exp, scale=-0.5).then_inc(done_sem, 1)

            act.wait_ge(s_w, 16 * n_weights)
            act.wait_ge(s_const, 2)
            nc.scalar.activation(c_silu[:, :], c_col[:, :], ACT.Silu).then_inc(s_csilu, 1)
            nc.scalar.preload_act_table_set("natural_log_exp_and_others")
            chain(nc.scalar.activation(knee_ln[:, :], ident[:, 0:1], ACT.Exp, scale=0.0, bias=neg_knee_col[:, :]))
            chain(nc.scalar.activation(knee_ln[:, :], knee_ln[:, :], ACT.Ln, bias=ones[:, 0:1]))
            nc.scalar.activation(a_neg[:, :, :], alog[:, :, :], ACT.Exp).then_inc(s_aexp, 1)

            for g in range(-1, GROUPS + 1):
                f, t = g + 1, g - 1
                front, tail = f < GROUPS, t >= 0
                fb, tb = f // CHUNKS, t // CHUNKS
                for s in range(STEPS):
                    k = g * STEPS + s
                    ke = k + AHEAD_EXP
                    if 0 <= ke < K:
                        ge, se = divmod(ke, STEPS)
                        n, half = divmod(se, HALVES)
                        if ke >= RD:
                            act.wait_ge(s_scan, ke - RD + 1)
                            gs, ss = divmod(ke - RD, STEPS)
                            if gs % CHUNKS < CHUNKS - 1:
                                nc.scalar.activation(state[:, ss:ss + 1], h[:, (ke - RD) % RH, T - 1:T],
                                                     ACT.Copy).then_inc(s_save, 1)
                        if se < HALVES:
                            act.wait_ge(s_delta, HALVES * ge + half + 1)
                        if ke == 0:
                            act.wait_ge(s_aneg, 1)
                        nc.scalar.activation(dA[:, ke % RD, :], delta[:, ge % 2, half, :], ACT.Exp,
                                             scale=a_neg[:, half, n:n + 1]).then_inc(s_dA, 1)
                    if front and s == F_STATS:
                        rstd(s_fvar, (f_rs, f_ve), f + 1, s_frs)
                    if front and s == F_TR:
                        j, bank = job("f", "tr", 0, f)
                        wait_job(act, j)
                        nc.scalar.activation(f_hT[:, :], bank[:, :], ACT.Identity, scale=mod_col[:, 1, fb:fb + 1],
                                             bias=mod_col[:, 0, fb:fb + 1]).then_inc(s_fhT, 1)
                        act.wait_ge(s_fhT, f + 1)
                        act.sem_inc(s_free["act"], 1)
                    if front and s in F_XP:
                        half = F_XP.index(s)
                        j, bank = job("f", "xp", half, f)
                        wait_job(act, j)
                        if f:
                            act.wait_ge(s_conv, HALVES * (f - 1) + half + 1)
                        nc.scalar.activation(xpad[:, half, HALO:HALO + T], bank[:, :], ACT.Copy).then_inc(s_xpad, 1)
                        nc.scalar.activation(zu[:, f % 2, HALVES + half, :], bank[:, :], ACT.Identity,
                                             scale=taps[:, half, HALO:TAPS],
                                             bias=cbias[:, half:half + 1]).then_inc(s_free["act"], 1)
                    if front and s in F_Z:
                        half = F_Z.index(s)
                        j, bank = job("f", "z", half, f)
                        wait_job(act, j)
                        if f >= 2:
                            act.wait_ge(s_gate, HALVES * (f - 2) + half + 1)
                        nc.scalar.activation(zu[:, f % 2, half, :], bank[:, :], ACT.Copy).then_inc(s_free["act"], 1)
                    if front and s == F_SILU:
                        act.wait_ge(s_conv, HALVES * (f + 1))
                        act.wait_ge(s_free["act"], freed_at[job("f", "z", 1, f)[0]][1])
                        nc.scalar.activation(zu[:, f % 2, :, :], zu[:, f % 2, :, :], ACT.Silu).then_inc(s_silu, 1)
                    if tail and s == T_STATS:
                        rstd(s_tvar, (t_rs, t_ve), t + 1, s_trs)
                    if tail and s == T_TR:
                        j, bank = job("t", "tr", 0, t)
                        wait_job(act, j)
                        nc.scalar.activation(t_hT[:, :], bank[:, :], ACT.Identity, scale=mod_col[:, 4, tb:tb + 1],
                                             bias=mod_col[:, 3, tb:tb + 1]).then_inc(s_thT, 1)
                        act.wait_ge(s_thT, t + 1)
                        act.sem_inc(s_free["act"], 1)
                    if tail and s == T_TANH:
                        for part in range(2):
                            j, bank = job("t", "node", part, t)
                            wait_job(act, j)
                            nc.scalar.activation(th[:, 2 * part:2 * part + 2, :],
                                                 bank[:, :].rearrange("p (i n) -> p i n", n=LEAVES), ACT.Tanh,
                                                 scale=0.5).then_inc(s_free["act"], 1)
                    if s == T_TANH:
                        nc.scalar.preload_act_table_set("natural_log_exp_and_others")
                    if tail and s == T_SIG:
                        act.wait_ge(s_free["act"], freed_at[job("t", "node", 1, t)[0]][1])
                        if t:
                            act.wait_ge(s_prob, t)
                        chain(nc.scalar.activation(go_l[:, :, :], th[:, :, :], ACT.Identity, scale=-0.5,
                                                   bias=half_col[:, :]))
                        nc.scalar.activation(go_r[:, :, :], th[:, :, :], ACT.Identity, scale=0.5,
                                             bias=half_col[:, :]).then_inc(s_sig, 1)
                    if front and s == F_XD:
                        j, bank = job("f", "xd", 0, f)
                        wait_job(act, j)
                        if f:
                            act.wait_ge(s_cst, 16 * f)
                            act.wait_ge(s_r2, f)
                            wait_job(act, job("f", "dt", 1, f - 1)[0])
                        nc.scalar.activation(xd[:, :], bank[:, :], ACT.Identity, bias=one_at[:, :]).then_inc(s_xd, 1)
                        act.wait_ge(s_xd, f + 1)
                        act.sem_inc(s_free["act"], 1)
                    if front and s == F_HI:
                        if f >= 2:
                            act.wait_ge(s_fill, (f - 1) * STEPS)
                        nc.scalar.activation(b_parts[:, f % 2, :], xd[:, :], ACT.Copy).then_inc(s_hi, 1)
                    if front and s == F_MID:
                        act.wait_ge(s_r1, f + 1)
                        nc.scalar.activation(b_parts[B_MID:P, f % 2, :], b_rest[B_MID:P, :],
                                             ACT.Copy).then_inc(s_mid, 1)
                    if front and s == F_LO:
                        act.wait_ge(s_r2, f + 1)
                        nc.scalar.activation(b_parts[B_LO:P, f % 2, :], b_rest[B_LO:P, :],
                                             ACT.Copy).then_inc(s_lo, 1)
                    if front and s == F_SP:
                        if f:
                            act.wait_ge(s_delta, HALVES * f)
                        for half in range(HALVES):
                            j, bank = job("f", "dt", half, f)
                            wait_job(act, j)
                            last = nc.scalar.activation(sp_abs[:, half, :], bank[:, :], ACT.Abs)
                        chain(last)
                        chain(nc.scalar.activation(sp_t[:, :, :], sp_abs[:, :, :], ACT.Relu,
                                                   bias=neg_knee_col[:, :]))
                        nc.scalar.activation(sp_e[:, :, :], sp_t[:, :, :], ACT.Exp, scale=-1.0,
                                             bias=neg_knee_col[:, :])
                        chain(nc.scalar.activation(sp_abs[:, :, :], sp_abs[:, :, :], ACT.Relu, scale=-1.0,
                                                   bias=knee_col[:, :]))
                        nc.scalar.activation(sp_t[:, :, :], sp_e[:, :, :], ACT.Identity, scale=-0.25,
                                             bias=third_col[:, :]).then_inc(s_poly, 1)
                        chain(nc.scalar.activation(sp_abs[:, :, :], sp_abs[:, :, :], ACT.Exp,
                                                   bias=neg_knee_col[:, :]))
                        nc.scalar.activation(sp_ln[:, :, :], sp_abs[:, :, :], ACT.Ln,
                                             bias=ones[:, 0:1]).then_inc(s_sp, 1)
                    if tail and s in T_PT:
                        part = T_PT.index(s)
                        j, bank = job("t", "pt", part, t)
                        wait_job(act, j)
                        if t:
                            wait_job(act, job("t", "ff", 0, t - 1)[0])
                        nc.scalar.activation(probT[:, part, :], bank[:, :], ACT.Copy).then_inc(s_pT, 1)
                        act.wait_ge(s_pT, 2 * t + part + 1)
                        act.sem_inc(s_free["act"], 1)

        @block.tensor
        def _(pe):
            def transpose(dst, src):
                return nc.tensor.transpose(dst, src, ident[:, :])

            pe.wait_ge(s_w, 16 * n_weights)
            pe.wait_ge(s_const, 2)
            pe.wait_ge(s_csilu, 1)
            for m in range(6):
                last = nc.tensor.matmul(mb[0][:, m * BATCH:(m + 1) * BATCH], w_mod[:, m, :], c_silu[:, :],
                                        start=True, stop=True)
            last.then_inc(s_pre_pe, 1)
            pe.wait_ge(s_cwide, 1)
            for b in range(BATCH):
                for i, m in enumerate((2, 5)):
                    last = nc.tensor.matmul(mb[1][:, (2 * b + i) * DM:(2 * b + i + 1) * DM], c_wide[:, b, :],
                                            w_mod[:, m, :], start=True, stop=True)
            last.then_inc(s_pre_pe, 1)
            for i in range(2):
                transpose(yb[0][:, i * P:(i + 1) * P], rout[:, i, :])
                last = transpose(yb[1][:, i * P:(i + 1) * P], leafv[:, i, :])
            last = transpose(yb[2][:, 0:P], wo[:, :])
            last.then_inc(s_pre_pe, 1)
            pe.wait_ge(s_pre_cp, 2)
            nc.tensor.matmul(bb[0][:, 0:2 * P], wq[:, :], rout_t[:, :], start=True, stop=True)
            for i in range(2):
                last = nc.tensor.matmul(bb[1][:, i * DM:(i + 1) * DM], leafv_t[:, i * P:(i + 1) * P], wo_t[:, :],
                                        start=True, stop=True)
            last.then_inc(s_pre_pe, 1)
            pe.wait_ge(s_wready, 1)

            def product(g, side, name, part):
                n, bank = job(side, name, part, g)
                b = g // CHUNKS
                wait_bank(pe, n)
                if (side, name) == ("f", "tr"):
                    pe.wait_ge(s_fxh, g + 1)
                    for i in range(TILES):
                        last = transpose(bank[:, i * P:(i + 1) * P], f_xhat[:, i, :])
                elif name in ("xp", "z"):
                    pe.wait_ge(s_fhT, g + 1)
                    col = (HALVES * (name == "z") + part) * P
                    last = nc.tensor.matmul(bank[:, :], w_in[:, col:col + P], f_hT[:, :], start=True, stop=True)
                elif name == "xd":
                    pe.wait_ge(s_silu, g + 1)
                    for hh in range(HALVES):
                        last = nc.tensor.matmul(bank[:, :], w_xp[:, hh, :], zu[:, g % 2, HALVES + hh, :],
                                                start=hh == 0, stop=hh == HALVES - 1)
                elif name == "dt":
                    pe.wait_ge(s_xd, g + 1)
                    last = nc.tensor.matmul(bank[:, :], w_dt[DT_ROW:ONE_ROW + 1, part * P:(part + 1) * P],
                                            xd[DT_ROW:ONE_ROW + 1, :], start=True, stop=True)
                elif name == "out":
                    pe.wait_ge(s_gate, HALVES * (g + 1))
                    for i in range(TILES):
                        for hh in range(HALVES):
                            last = nc.tensor.matmul(bank[:, i * P:(i + 1) * P], yg[:, hh, i * P:(i + 1) * P],
                                                    w_out_g[:, b, hh, :], start=hh == 0, stop=hh == HALVES - 1)
                elif (side, name) == ("t", "tr"):
                    pe.wait_ge(s_txh, g + 1)
                    for i in range(TILES):
                        last = transpose(bank[:, i * P:(i + 1) * P], t_xhat[:, i, :])
                elif name == "node":
                    pe.wait_ge(s_thT, g + 1)
                    for i in range(2):
                        tile = 2 * part + i
                        last = nc.tensor.matmul(bank[:, i * LEAVES:(i + 1) * LEAVES],
                                                t_hT[:, tile * P:(tile + 1) * P], w_node[:, :],
                                                start=True, stop=True)
                elif name == "pt":
                    pe.wait_ge(s_prob, g + 1)
                    for i in range(TILES):
                        last = transpose(bank[:, i * P:(i + 1) * P],
                                         prob[(DEPTH - 1) % 2][:, i, part * P:(part + 1) * P])
                else:
                    pe.wait_ge(s_pT, 2 * (g + 1))
                    for i in range(TILES):
                        dst = bank[:, i * P:(i + 1) * P]
                        nc.tensor.matmul(dst, ones[0:1, :], wo_b_g[0:1, b, :], start=True, stop=False)
                        for hh in range(2):
                            last = nc.tensor.matmul(dst, probT[:, hh, i * P:(i + 1) * P], leaf_out_g[:, b, hh, :],
                                                    start=False, stop=hh == 1)
                last.then_inc(s_job, 1)

            for g in range(-1, GROUPS + 1):
                for s in range(STEPS):
                    k = g * STEPS + s
                    kf, ks = k + AHEAD_FILL, k - LAG_SUM
                    if 0 <= kf < K:
                        gf, sf = divmod(kf, STEPS)
                        if sf == 0:
                            pe.wait_ge(s_lo, gf + 1)
                        if kf >= RB:
                            pe.wait_ge(s_scan, kf - RB + 1)
                        nc.tensor.matmul(bb[kf % RB][:, :], sel[:, sf // HALVES, :], b_parts[:, gf % 2, :],
                                         start=True, stop=True).then_inc(s_fill, 1)
                    if 0 <= ks < K:
                        gs, ss = divmod(ks, STEPS)
                        n, half = divmod(ss, HALVES)
                        hg = HALVES * gs + half
                        bank = yb[hg % RY]
                        if n == 0:
                            if hg >= RY:
                                pe.wait_ge(s_gate, hg - RY + 1)
                            nc.tensor.matmul(bank[:, :], diag_d[:, half, :], zu[:, gs % 2, HALVES + half, :],
                                             start=True, stop=False)
                        pe.wait_ge(s_hc, ks + 1)
                        nc.tensor.matmul(bank[:, :], ident[:, :], hc[:, ks % RH, :],
                                         start=False, stop=n == N - 1).then_inc(s_sum, 1)
                    for side, name, part, at in JOBS:
                        own = g + 1 if side == "f" else g - 1
                        if at == s and 0 <= own < GROUPS:
                            product(own, side, name, part)

        @block.vector
        def _(dve):
            seq = 0

            def chain(ins):
                nonlocal seq
                seq += 1
                ins.then_inc(s_dseq, 1)
                dve.wait_ge(s_dseq, seq)

            v = nc.vector
            dve.wait_ge(s_w, 16 * n_weights)
            dve.wait_ge(s_const, 2)
            dve.wait_ge(s_csilu, 1)
            for b in range(BATCH):
                last = v.tensor_scalar(c_wide[:, b, :], ones[:, :], c_silu[:, b:b + 1], None, ALU.mult)
            last.then_inc(s_cwide, 1)
            for hh in range(HALVES):
                v.tensor_scalar(diag_d[:, hh, :], ident[:, :], dskip[:, hh:hh + 1], None, ALU.mult)
            dve.wait_ge(s_aexp, 1)
            v.tensor_scalar(a_neg[:, :, :], a_neg[:, :, :], -1.0, None, ALU.mult).then_inc(s_aneg, 1)
            dve.wait_ge(s_pre_pe, 1)
            chain(v.tensor_copy(mod_col[:, :, :], mb[0][:, 0:6 * BATCH].rearrange("p (m b) -> p m b", b=BATCH)))
            for m in (1, 4):
                v.tensor_scalar(mod_col[:, m, :], mod_col[:, m, :], 1.0, None, ALU.add)
            dve.wait_ge(s_pre_pe, 2)
            chain(v.tensor_copy(gate_raw[:, :, :, :],
                                mb[1][:, :].rearrange("p (b i d) -> p b i d", b=BATCH, i=2)))
            v.tensor_scalar(gate_sgn[:, :, :, :], gate_raw[:, :, :, :], 0.0, 2.0, ALU.is_ge, ALU.mult)
            chain(v.scalar_tensor_tensor(gate_abs[:, :, :, :], gate_raw[:, :, :, :], -1.0, gate_raw[:, :, :, :],
                                         ALU.mult, ALU.max))
            chain(v.tensor_scalar(gate_abs[:, :, :, :], gate_abs[:, :, :, :], GATE_MIN, None, ALU.max))
            chain(v.scalar_tensor_tensor(gate_raw[:, :, :, :], gate_sgn[:, :, :, :], -1.0, gate_abs[:, :, :, :],
                                         ALU.add, ALU.mult))
            dve.wait_ge(s_pre_pe, 3)
            v.tensor_copy(rout_t[:, :], yb[0][:, 0:2 * P])
            v.tensor_copy(wo_t[:, :], yb[2][:, 0:P]).then_inc(s_pre_cp, 1)
            v.tensor_copy(leafv_t[:, :], yb[1][:, 0:2 * P]).then_inc(s_pre_cp, 1)
            dve.wait_ge(s_pre_pe, 4)
            v.tensor_copy(w_node[:, :], bb[0][:, 0:2 * P])
            chain(v.tensor_copy(leaf_out[:, :, :], bb[1][:, 0:2 * DM].rearrange("p (i d) -> p i d", d=DM)))
            for b in range(BATCH):
                for i in range(2):
                    v.tensor_tensor(w_out_g[:, b, i, :], w_out[:, i, :], gate_raw[:, b, 0, :], ALU.mult)
                    v.tensor_tensor(leaf_out_g[:, b, i, :], leaf_out[:, i, :], gate_raw[:, b, 1, :], ALU.mult)
                last = v.tensor_tensor(wo_b_g[0:1, b, :], wo_b[0:1, :], gate_raw[0:1, b, 1, :], ALU.mult)
            last.then_inc(s_wready, 1)

            def stats(g, bn, mv, ve, ready):
                for i in range(TILES):
                    last = v.bn_stats(bn[:, i, :], xs[:, g * TILES + i, :])
                chain(last)
                for i in range(TILES):
                    last = v.bn_aggr(mv[:, i, :], bn[:, i, :])
                chain(last)
                v.tensor_scalar(ve[:, :], mv[:, :, 1], EPS, None, ALU.add).then_inc(ready, 1)

            def normalise(g, mv, rs, rs_ready, xhat, ready):
                dve.wait_ge(rs_ready, g + 1)
                for i in range(TILES):
                    last = v.tensor_scalar(xhat[:, i, :], xs[:, g * TILES + i, :], mv[:, i, 0:1], rs[:, i:i + 1],
                                           ALU.subtract, ALU.mult)
                last.then_inc(ready, 1)

            for g in range(-1, GROUPS + 1):
                f, t = g + 1, g - 1
                front, tail = f < GROUPS, t >= 0
                for s in range(STEPS):
                    k = g * STEPS + s
                    kd = k + AHEAD_DBU
                    if 0 <= kd < K:
                        gd, sd = divmod(kd, STEPS)
                        half = sd % HALVES
                        if sd < HALVES:
                            dve.wait_ge(s_du, HALVES * gd + half + 1)
                        dve.wait_ge(s_fill, kd + 1)
                        v.tensor_tensor(bb[kd % RB][:, :], du[:, gd % 2, half, :], bb[kd % RB][:, :],
                                        ALU.mult).then_inc(s_dbu, 1)
                    if 0 <= k < K:
                        dve.wait_ge(s_dA, k + 1)
                        dve.wait_ge(s_dbu, k + 1)
                        if k >= RH:
                            dve.wait_ge(s_hc, k - RH + 1)
                            if saves(k - RH + 1):
                                dve.wait_ge(s_save, saves(k - RH + 1))
                        start = state[:, s:s + 1] if g % CHUNKS else 0.0
                        v.tensor_tensor_scan(h[:, k % RH, :], dA[:, k % RD, :], bb[k % RB][:, :], start,
                                             ALU.mult, ALU.add).then_inc(s_scan, 1)
                    if front and s == F_STATS:
                        dve.wait_ge(s_x, 16 * GROUPS if f else 16)
                        stats(f, f_bn, f_mv, f_ve, s_fvar)
                    if front and s == F_XHAT:
                        if f:
                            wait_job(dve, job("f", "tr", 0, f - 1)[0])
                        normalise(f, f_mv, f_rs, s_frs, f_xhat, s_fxh)
                    if front and s in F_CONV:
                        half = F_CONV.index(s)
                        acc = zu[:, f % 2, HALVES + half, :]
                        dve.wait_ge(s_xpad, HALVES * f + half + 1)
                        dve.wait_ge(s_free["act"], freed_at[job("f", "xp", half, f)[0]][1])
                        for tap in range(HALO):
                            chain(v.scalar_tensor_tensor(acc, xpad[:, half, tap:tap + T], taps[:, half, tap:tap + 1],
                                                         acc, ALU.mult, ALU.add))
                        if (f + 1) % CHUNKS:
                            last = v.tensor_copy(xpad[:, half, 0:HALO], xpad[:, half, T:T + HALO])
                        else:
                            last = v.memset(xpad[:, half, 0:HALO], 0.0)
                        last.then_inc(s_conv, 1)
                    if front and s in F_POLY:
                        if s == F_POLY[0]:
                            dve.wait_ge(s_poly, f + 1)
                            chain(v.tensor_tensor(sp_t[:, :, :], sp_t[:, :, :], sp_e[:, :, :], ALU.mult))
                            chain(v.scalar_tensor_tensor(sp_t[:, :, :], sp_t[:, :, :], -0.5, sp_e[:, :, :],
                                                         ALU.add, ALU.mult))
                        else:
                            chain(v.scalar_tensor_tensor(sp_t[:, :, :], sp_t[:, :, :], 1.0, sp_e[:, :, :],
                                                         ALU.add, ALU.mult))
                            dve.wait_ge(s_sp, f + 1)
                            chain(v.scalar_tensor_tensor(sp_ln[:, :, :], sp_ln[:, :, :], knee_ln[:, :],
                                                         sp_t[:, :, :], ALU.subtract, ALU.add))
                    if front and s == F_DELTA:
                        for half in range(HALVES):
                            j, bank = job("f", "dt", half, f)
                            v.scalar_tensor_tensor(delta[:, f % 2, half, :], bank[:, :], 0.0, sp_ln[:, half, :],
                                                   ALU.max, ALU.add).then_inc(s_delta, 1)
                        dve.wait_ge(s_delta, HALVES * (f + 1))
                        dve.sem_inc(s_free["dve"], 2)
                    if tail and s in T_GATE:
                        half = T_GATE.index(s)
                        hg = HALVES * t + half
                        dve.wait_ge(s_sum, t * STEPS + STEPS - HALVES + half + 1)
                        if t:
                            wait_job(dve, job("t", "out", 0, t - 1)[0])
                        v.tensor_tensor(yg[:, half, :], yb[hg % RY][:, :], zu[:, t % 2, half, :],
                                        ALU.mult).then_inc(s_gate, 1)
                    if tail and s == T_ADD:
                        j, bank = job("t", "out", 0, t)
                        wait_job(dve, j)
                        x1 = xs[:, t * TILES:(t + 1) * TILES, :]
                        v.tensor_tensor(x1, bank[:, :].rearrange("p (i d) -> p i d", d=DM), x1,
                                        ALU.add).then_inc(s_free["dve"], 1)
                        dve.wait_ge(s_free["dve"], freed_at[j][1])
                    if tail and s == T_STATS:
                        stats(t, t_bn, t_mv, t_ve, s_tvar)
                    if tail and s == T_XHAT:
                        if t:
                            wait_job(dve, job("t", "tr", 0, t - 1)[0])
                        normalise(t, t_mv, t_rs, s_trs, t_xhat, s_txh)
                    if tail and s == T_FIN:
                        j, bank = job("t", "ff", 0, t)
                        wait_job(dve, j)
                        x1 = xs[:, t * TILES:(t + 1) * TILES, :]
                        v.tensor_tensor(x1, bank[:, :].rearrange("p (i d) -> p i d", d=DM), x1,
                                        ALU.add).then_inc(s_fin, 1)
                        dve.wait_ge(s_fin, t + 1)
                        dve.sem_inc(s_free["dve"], 1)


_INS = ["L0_attn_x", "L0_attn_W_in", "L0_attn_conv_w", "L0_attn_conv_b", "L0_attn_W_xp", "L0_attn_W_dt",
        "L0_attn_dt_bias", "L0_attn_A_log", "L0_attn_D_skip", "L0_attn_W_out", "L0_ffn_Wq", "L0_ffn_routers",
        "L0_ffn_leaf_values", "L0_ffn_Wout_w", "L0_ffn_Wout_b", "L0_c", "L0_wmod"]
_OUTS = [((2, 2048, 128), "float32")]


def kernel(**inputs):
    import numpy as _np
    import concourse.bacc as _bacc
    from concourse import mybir as _mybir
    from concourse.bass_utils import run_bass_kernel_spmd as _run

    nc = _bacc.Bacc("TRN2", target_bir_lowering=False, num_devices=1)
    arrays, args = {}, []
    for name in _INS:
        a = _np.ascontiguousarray(inputs[name])
        arrays[f"in_{name}_dram"] = a
        args.append(nc.dram_tensor(f"in_{name}_dram", a.shape, _mybir.dt.from_np(a.dtype), kind="ExternalInput").ap())
    for i, (shape, dtype) in enumerate(_OUTS):
        dt = _mybir.dt.from_np(_np.dtype(dtype))
        args.append(nc.dram_tensor(f"out_{i}_dram", shape, dt, kind="ExternalOutput").ap())
    bass_adaln_mamba_tree_ffn_kernel(nc, *args)
    r = _run(nc, [arrays], core_ids=[0])
    got = tuple(r.results[0][f"out_{i}_dram"] for i in range(len(_OUTS)))
    return got[0]
```

```python
import math

import concourse.bass as bass
from concourse import mybir
from contextlib import ExitStack


def bass_adaln_mamba_tree_ffn_kernel(
    nc: bass.Bass,
    x: bass.AP,
    W_in: bass.AP,
    conv_w: bass.AP,
    conv_b: bass.AP,
    W_xp: bass.AP,
    W_dt: bass.AP,
    dt_bias: bass.AP,
    A_log: bass.AP,
    D_skip: bass.AP,
    W_out: bass.AP,
    Wq: bass.AP,
    routers: bass.AP,
    leaf_values: bass.AP,
    Wo: bass.AP,
    Wo_b: bass.AP,
    c: bass.AP,
    wmod: bass.AP,
    out: bass.AP,
):
    f32 = mybir.dt.float32
    bf16 = mybir.dt.bfloat16
    ALU = mybir.AluOpType
    ACT = mybir.ActivationFunctionType

    P = 128
    BATCH, L, DM = x.shape
    DI = W_out.shape[0]
    HALVES = DI // P
    R = W_dt.shape[0]
    N = (W_xp.shape[1] - R) // 2
    TAPS = conv_w.shape[2]
    HALO = TAPS - 1
    T = 512
    TILES = T // P
    CHUNKS = L // T
    GROUPS = BATCH * CHUNKS
    STEPS = N * HALVES
    K = GROUPS * STEPS
    NODES = routers.shape[0]
    LEAVES = leaf_values.shape[0]
    DEPTH = LEAVES.bit_length() - 1
    EPS = 1e-5
    THETA = 2.0 ** -5
    KNEE = -math.log(THETA)
    GATE_MIN = 0.25
    QUARTERS = 4
    NQ = N // QUARTERS
    B_HI, C_ROW, B_MID, B_LO = 0, N, 64, 96

    PAIRS = K // HALVES
    RB, RY, RD, RP, RW = 3, HALVES, 5, 4, 2
    RM = {"f": 2, "t": 1}
    AHEAD_EXP, AHEAD_FILL, AHEAD_DBU, LAG_SUM = 4, 5, 2, 5

    N_STATS, N_XHAT = 5, 7
    F_SILU, F_ABS, F_SP, F_POLY, F_DELTA, F_DU = 10, (13, 15), (16, 17, 18, 19, 20, 21), (20, 21, 23), 24, (25, 26)
    F_HI, F_R1, F_MID, F_R2, F_LO = 18, 19, 21, 22, 24
    T_GATE, T_ADD, T_STATS, T_RSTD, T_XHAT = ((4, 5), (4, 5)), (13, 11), (14, 12), (15, 13), (17, 14)
    U_TANH, U_SIG, U_LEAF = (F_SILU, 0), ((11, 12), (1, 2)), ((13, 14, 15, 16, 17, 18), (3, 4, 5, 6, 7, 8))
    U_FIN = (27, 26)

    JOBS = {
        "f": {("xp", 0): (1, (0, 1), ()), ("xp", 1): (1, (2, 3), ()), ("z", 0): (1, (7,), ()),
              ("z", 1): (1, (8,), ()), ("dt", 0): (1, (11, 12), ()), ("dt", 1): (1, (13, 14), ()),
              ("xd", 0): (1, (15, 16), ()), ("tr", 0): (2, (28,), ())},
        "t": {("yt", 0): (-1, (6,), (6,)), ("yt", 1): (-1, (8,), (8,)), ("out", 0): (-1, (10, 11), (10,)),
              ("tr", 0): (-1, (19,), (15,)), ("pt", 0): (-2, (21,), (21,)), ("pt", 1): (-2, (23,), (23,)),
              ("ff", 0): (-2, (25, 26), (25,)), ("node", 0): (-1, (28,), (17,)),
              ("node", 1): (-1, (30,), (19,))},
    }
    BY_DVE = {"out", "ff"}
    FIRST, LAST = -2, GROUPS + 1
    job_at, read_at, reads = {}, {"f": [], "t": []}, {}
    for side in JOBS:
        for g in range(FIRST, LAST + 1):
            for (name, part), (off, *steps) in sorted(JOBS[side].items(), key=lambda job: job[1][1 + (g >= GROUPS)]):
                if 0 <= g + off < GROUPS:
                    job_at[side, name, part, g + off] = len(read_at[side])
                    by = "dve" if name in BY_DVE else "act"
                    reads[side, by] = reads.get((side, by), 0) + 1
                    read_at[side].append((side, by, reads[side, by]))

    ctx = ExitStack()
    with ctx:
        def sb(name, shape, dt=f32):
            return ctx.enter_context(nc.sbuf_tensor(name, shape, dt))

        def sem(name):
            return ctx.enter_context(nc.semaphore(name))

        ident = sb("ident", [P, P])
        sel = sb("sel", [P, N, P], bf16)
        ones = sb("ones", [P, P])
        half_col = sb("half_col", [P, 1])
        neg_third_col = sb("neg_third_col", [P, 1])
        knee_col = sb("knee_col", [P, 1])
        neg_knee_col = sb("neg_knee_col", [P, 1])
        knee_ln = sb("knee_ln", [P, 1])
        w_in = sb("w_in", [P, 2 * DI])
        w_xp = sb("w_xp", [P, HALVES, P])
        w_dt = sb("w_dt", [R, DI])
        dtb = sb("dtb", [P, HALVES])
        w_xdt = sb("w_xdt", [P, HALVES, DI])
        w_out = sb("w_out", [P, HALVES, DM])
        wq = sb("wq", [P, DM])
        wo_b = sb("wo_b", [1, DM])
        w_conv = sb("w_conv", [P, TAPS, DI])
        zeros = sb("zeros", [P, HALO])
        cbias = sb("cbias", [P, HALVES])
        dskip = sb("dskip", [P, HALVES])
        alog = sb("alog", [P, HALVES, N])
        a_neg = sb("a_neg", [P, HALVES, N])
        c_col = sb("c_col", [P, BATCH])
        c_silu = sb("c_silu", [P, BATCH])
        c_wide = sb("c_wide", [P, BATCH, P])
        mod_col = sb("mod_col", [P, 6, BATCH])
        rout_t = sb("rout_t", [P, 2 * P])
        leafv_t = sb("leafv_t", [P, 2 * P])
        wo_t = sb("wo_t", [P, DM])
        w_node = sb("w_node", [P, 2 * P])
        leaf_out = sb("leaf_out", [P, 2, DM])
        w_out_g = sb("w_out_g", [P, BATCH, HALVES, DM])
        leaf_out_g = sb("leaf_out_g", [P, BATCH, 2, DM])
        wo_b_g = sb("wo_b_g", [1, BATCH, DM])
        diag_d = sb("diag_d", [P, HALVES, P])
        xs = sb("xs", [P, GROUPS * TILES, DM])
        dA = sb("dA", [P, RD, T])
        dbu = sb("dbu", [P, RW, HALVES, T])
        h = sb("h", [P, RP, HALVES, T])
        state = sb("state", [P, N, HALVES])
        c_rows = sb("c_rows", [P, QUARTERS, NQ, T])
        zu = sb("zu", [P, 2, 2 * HALVES, T])
        delta = sb("delta", [P, 2, HALVES, T])
        du = sb("du", [P, 2, HALVES, T])
        b_parts = sb("b_parts", [P, 2, T], bf16)
        f_bn = sb("f_bn", [P, TILES, 6])
        f_mv = sb("f_mv", [P, TILES, 2])
        f_ve = sb("f_ve", [P, TILES])
        f_rs = sb("f_rs", [P, TILES])
        f_xhat = sb("f_xhat", [P, TILES, DM])
        f_hT = sb("f_hT", [P, HALO + T])
        xd = sb("xd", [P, T])
        b_rest = sb("b_rest", [P, T])
        sp_abs = sb("sp_abs", [P, HALVES, T])
        sp_e = sb("sp_e", [P, HALVES, T])
        sp_t = sb("sp_t", [P, HALVES, T])
        sp_ln = sb("sp_ln", [P, HALVES, T])
        yg = sb("yg", [P, HALVES, T])
        ygT = sb("ygT", [P, HALVES, T])
        t_bn = sb("t_bn", [P, TILES, 6])
        t_mv = sb("t_mv", [P, TILES, 2])
        t_ve = sb("t_ve", [P, TILES])
        t_rs = sb("t_rs", [P, TILES])
        t_xhat = sb("t_xhat", [P, TILES, DM])
        t_hT = sb("t_hT", [P, T])
        go_r = sb("go_r", [P, TILES, LEAVES])
        go_l = sb("go_l", [P, TILES, LEAVES])
        prob = [sb("prob_even", [P, TILES, LEAVES // 2]), sb("prob_odd", [P, TILES, LEAVES])]
        probT = sb("probT", [P, 2, T])
        taps = ygT[:, :, :].rearrange("p a (b k) -> p (a b) k", k=TAPS)
        rout = yg[:, 0, 0:2 * DM].rearrange("p (i d) -> p i d", i=2)
        leafv = yg[:, 0, 2 * DM:4 * DM].rearrange("p (i d) -> p i d", i=2)
        wo = yg[:, 1, 0:DM]
        w_dtin = yg[:, 1, DM:DM + HALVES * R].rearrange("p (h r) -> p h r", h=HALVES)
        w_dtin_t = t_xhat[0:R, 0:HALVES, :].rearrange("r h e -> r (h e)")
        w_mod = probT[:, :, :].rearrange("p a t -> p (a t)")[:, 0:6 * DM].rearrange("p (j d) -> p j d", j=6)
        gate_raw = prob[0][:, :, :].rearrange("p i n -> p (i n)").rearrange("p (b i d) -> p b i d", b=BATCH, i=2)
        gate_sgn = prob[1][:, 0:BATCH, :].rearrange("p b (i d) -> p b i d", i=2)
        gate_abs = prob[1][:, BATCH:2 * BATCH, :].rearrange("p b (i d) -> p b i d", i=2)

        bb = [ctx.enter_context(nc.psum_tensor(f"bb{i}", [P, T], f32)) for i in range(RB)]
        yb = [ctx.enter_context(nc.psum_tensor(f"yb{i}", [P, T], f32)) for i in range(RY)]
        mb = {side: [ctx.enter_context(nc.psum_tensor(f"m{side}{i}", [P, T], f32)) for i in range(RM[side])]
              for side in RM}
        c_dram = nc.dram_tensor("c_dram", [GROUPS, N, T], f32, kind="Internal").ap()

        s_w = sem("weights_loaded")
        s_x0 = sem("x_of_group_0_loaded")
        s_x = sem("x_of_other_groups_loaded")
        s_rt = sem("rout_zeroed")
        s_wz = sem("w_xp_zeroed")
        s_const = sem("constants_made")
        s_pool = sem("pool_seq")
        s_dseq = sem("dve_seq")
        s_aseq = sem("act_seq")
        s_pre_pe = sem("pre_products")
        s_pre_cp = sem("pre_copied")
        s_csilu = sem("c_silu_ready")
        s_cwide = sem("c_wide_ready")
        s_aexp = sem("a_exp_ready")
        s_aneg = sem("a_neg_ready")
        s_wready = sem("scaled_weights_ready")
        s_fill = sem("b_filled")
        s_dbu = sem("dbu_done")
        s_dA = sem("dA_done")
        s_scan = sem("scan_done")
        s_save = sem("state_saved")
        s_hc = sem("hc_done")
        s_sum = sem("sum_done")
        s_job = {"f": sem("f_product_done"), "t": sem("t_product_done")}
        s_read = {("f", "act"): sem("f_product_read_by_act"), ("t", "act"): sem("t_product_read_by_act"),
                  ("t", "dve"): sem("t_product_read_by_dve")}
        s_halo = sem("halo_ready")
        s_wfront = sem("front_weights_loaded")
        s_wconv = sem("conv_weights_ready")
        s_wdtt = sem("dt_weights_transposed")
        s_wdtc = sem("dt_weights_copied")
        s_wdtp = sem("dt_weights_multiplied")
        s_wdt = sem("dt_weights_ready")
        s_modc = sem("mod_columns_ready")
        s_leafL = sem("leaf_left_ready")
        s_fvar = sem("f_var_ready")
        s_frs = sem("f_rstd_ready")
        s_fxh = sem("f_xhat_ready")
        s_silu = sem("silu_done")
        s_hi = sem("b_hi_ready")
        s_r1 = sem("b_rest1_ready")
        s_mid = sem("b_mid_ready")
        s_r2 = sem("b_rest2_ready")
        s_lo = sem("b_parts_ready")
        s_poly = sem("softplus_series_ready")
        s_sp = sem("softplus_ln_ready")
        s_delta = sem("delta_ready")
        s_du = sem("du_ready")
        s_cst = sem("c_stored")
        s_cld = [sem(f"c_loaded{q}") for q in range(QUARTERS)]
        s_gate = sem("y_gated")
        s_tvar = sem("t_var_ready")
        s_trs = sem("t_rstd_ready")
        s_txh = sem("t_xhat_ready")
        s_tanh = sem("node_tanh_ready")
        s_sig = sem("node_sigmoids_ready")
        s_prob = sem("leaf_probs_ready")
        s_out = sem("out_stored")

        block = ctx.enter_context(nc.Block())

        def job(side, name, part, g):
            n = job_at[side, name, part, g]
            return n, mb[side][n % RM[side]]

        def read_step(side, name, part, late):
            return JOBS[side][name, part][1 + late][-1] + 1

        def wait_job(eng, side, name, part, g):
            eng.wait_ge(s_job[side], job_at[side, name, part, g] + 1)

        def wait_read(eng, side, name, part, g):
            _, by, count = read_at[side][job_at[side, name, part, g]]
            eng.wait_ge(s_read[side, by], count)

        def wait_bank(eng, side, n):
            if n >= RM[side]:
                _, by, count = read_at[side][n - RM[side]]
                eng.wait_ge(s_read[side, by], count)

        def saves(pair):
            g, n = divmod(pair, N)
            return (g // CHUNKS) * (CHUNKS - 1) * N + (g % CHUNKS) * N + (n if saved(pair) else 0)

        def saved(pair):
            return pair // N % CHUNKS < CHUNKS - 1

        n_front, n_rest = 12, 9

        @block.sync
        def _(sp):
            count = {s_wfront: 0, s_w: 0}

            def load(dst, src, which=s_w):
                count[which] += 1
                sp.dma_start(dst, src, allow_slow_non_contiguous=True).then_inc(which, 16)

            def load_x(g):
                b, ch = divmod(g, CHUNKS)
                sp.dma_start(xs[:, g * TILES:(g + 1) * TILES, :],
                             x[b, ch * T:(ch + 1) * T, :].rearrange("(i p) d -> p i d", p=P)).then_inc(s_x if g else s_x0, 16)

            load_x(0)
            load(c_col[:, :], c.rearrange("b k -> k b"), s_wfront)
            load(w_mod[:, :, :], wmod.rearrange("k (j d) -> k j d", j=6), s_wfront)
            load(w_in[:, :], W_in, s_wfront)
            load(taps[:, :, :].rearrange("p e k -> p (e k)"),
                 conv_w.rearrange("e o k -> (e o k)").partition_broadcast(P), s_wfront)
            load(cbias[:, :], conv_b.rearrange("(h p) -> p h", p=P), s_wfront)
            sp.wait_ge(s_wz, 1)
            xp_v = W_xp.rearrange("(h p) j -> p h j", p=P)
            for row, first, width in ((B_HI, R, N), (C_ROW, R + N, N), (B_MID, R, N), (B_LO, R, N)):
                load(w_xp[:, :, row:row + width], xp_v[:, :, first:first + width], s_wfront)
            load(w_dt[:, :], W_dt, s_wfront)
            load(dtb[:, :], dt_bias.rearrange("(h p) -> p h", p=P), s_wfront)
            load(w_dtin[:, :, :], xp_v[:, :, 0:R], s_wfront)
            load(alog[:, :, :], A_log.rearrange("(h p) n -> p h n", p=P))
            load(dskip[:, :], D_skip.rearrange("(h p) -> p h", p=P))
            load(w_out[:, :, :], W_out.rearrange("(h p) d -> p h d", p=P))
            load(wq[:, :], Wq)
            load(leafv[:, :, :], leaf_values.rearrange("(h p) d -> p h d", p=P))
            load(wo, Wo)
            load(wo_b[:, :], Wo_b.rearrange("(a n) -> a n", a=1))
            sp.wait_ge(s_rt, 1)
            load(rout[:, 0, :], routers[0:P, :])
            load(rout[0:NODES - P, 1, :], routers[P:NODES, :])
            assert (count[s_wfront], count[s_w]) == (n_front, n_rest)
            for g in range(1, GROUPS):
                load_x(g)

            for g in range(-1, LAST + 1):
                f, u = g + 1, g - 2
                if f < GROUPS:
                    wait_read(sp, "f", "xd", 0, f)
                    sp.dma_start(c_dram[f, :, :], xd[C_ROW:C_ROW + N, :]).then_inc(s_cst, 16)
                    sp.wait_ge(s_cst, 16 * (f + 1))
                    for q in range(QUARTERS):
                        if g >= 0:
                            sp.wait_ge(s_hc, g * N + (q + 1) * NQ)
                        src = c_dram[f, q * NQ:(q + 1) * NQ, :].rearrange("n t -> (n t)")
                        sp.dma_start(c_rows[:, q, :, :].rearrange("p n t -> p (n t)"),
                                     src.partition_broadcast(P)).then_inc(s_cld[q], 16)
                if u >= 0:
                    b, ch = divmod(u, CHUNKS)
                    wait_read(sp, "t", "ff", 0, u)
                    sp.dma_start(out[b, ch * T:(ch + 1) * T, :].rearrange("(i p) d -> p i d", p=P),
                                 xs[:, u * TILES:(u + 1) * TILES, :]).then_inc(s_out, 16)
            sp.wait_ge(s_out, 16 * GROUPS)

        @block.gpsimd
        def _(pool):
            seq = 0

            def chain(ins):
                nonlocal seq
                seq += 1
                ins.then_inc(s_pool, 1)
                pool.wait_ge(s_pool, seq)

            nc.gpsimd.memset(w_xp[:, :, :], 0.0).then_inc(s_wz, 1)
            nc.gpsimd.memset(rout[:, 1, :], 0.0).then_inc(s_rt, 1)
            chain(nc.gpsimd.memset(ident[:, :], 0.0))
            chain(nc.gpsimd.affine_select(out=ident[:, :], in_=ident[:, :], compare_op=ALU.not_equal, fill=1.0,
                                          base=0, pattern=[[-1, P]], channel_multiplier=1))
            nc.gpsimd.memset(half_col[:, :], 0.5)
            nc.gpsimd.memset(neg_third_col[:, :], -1.0 / 3.0)
            nc.gpsimd.memset(knee_col[:, :], KNEE)
            nc.gpsimd.memset(neg_knee_col[:, :], -KNEE)
            chain(nc.gpsimd.memset(ones[:, :], 1.0))
            nc.gpsimd.memset(zeros[:, :], 0.0).then_inc(s_const, 1)
            chain(nc.gpsimd.memset(sel[:, :, :], 0.0))
            for first in (B_HI, B_MID, B_LO):
                chain(nc.gpsimd.affine_select(out=sel[:, :, :], in_=sel[:, :, :], compare_op=ALU.not_equal,
                                              fill=1.0, base=-first, pattern=[[-1, N], [0, P]],
                                              channel_multiplier=1))
            nc.gpsimd.memset(half_col[:, :], 0.5).then_inc(s_const, 1)

            def leaf_products(level, side):
                n = 1 << level
                dst = prob[level % 2][:, :, 0:2 * n].rearrange("p i (n two) -> p i n two", two=2)[:, :, :, side]
                node = (go_l, go_r)[side][:, :, n - 1:2 * n - 1]
                if level == 0:
                    return nc.gpsimd.tensor_copy(dst, node)
                return nc.gpsimd.tensor_tensor(dst, prob[(level + 1) % 2][:, :, 0:n], node, ALU.mult)

            for g in range(-1, LAST + 1):
                f, u, late = g + 1, g - 2, g >= GROUPS
                front, leaf = f < GROUPS, 0 <= u < GROUPS
                for s in range(STEPS):
                    if 0 <= g < GROUPS and s % HALVES == HALVES - 1:
                        n = s // HALVES
                        pair, q = g * N + n, n // NQ
                        if n % NQ == 0:
                            pool.wait_ge(s_cld[q], 16 * (g + 1))
                        pool.wait_ge(s_scan, HALVES * (pair + 1))
                        if saved(pair):
                            pool.wait_ge(s_save, saves(pair) + 1)
                        hp = h[:, pair % RP, :, :]
                        nc.gpsimd.tensor_tensor(hp, hp, c_rows[:, q, n % NQ, :].unsqueeze(1).broadcast_to([P, HALVES, T]),
                                                ALU.mult).then_inc(s_hc, 1)
                    if front and s == F_R1:
                        pool.wait_ge(s_hi, f + 1)
                        nc.gpsimd.tensor_tensor(b_rest[:, :], xd[:, :], b_parts[:, f % 2, :],
                                                ALU.subtract).then_inc(s_r1, 1)
                    if front and s == F_R2:
                        pool.wait_ge(s_r1, f + 1)
                        pool.wait_ge(s_mid, f + 1)
                        nc.gpsimd.tensor_tensor(b_rest[:, :], b_rest[:, :], b_parts[:, f % 2, :],
                                                ALU.subtract).then_inc(s_r2, 1)
                    if front and s in F_DU:
                        half = F_DU.index(s)
                        pool.wait_ge(s_delta, HALVES * f + half + 1)
                        pool.wait_ge(s_silu, f + 1)
                        nc.gpsimd.tensor_tensor(du[:, f % 2, half, :], delta[:, f % 2, half, :],
                                                zu[:, f % 2, HALVES + half, :], ALU.mult).then_inc(s_du, 1)
                    if leaf and s in U_LEAF[late]:
                        at = U_LEAF[late].index(s)
                        if at == 0:
                            pool.wait_ge(s_sig, u + 1)
                            for level in range(DEPTH - 4):
                                chain(leaf_products(level, 0))
                                chain(leaf_products(level, 1))
                        elif at < 4:
                            chain(leaf_products(DEPTH - 5 + at, 0))
                            chain(leaf_products(DEPTH - 5 + at, 1))
                        elif at == 4:
                            if u:
                                wait_job(pool, "t", "pt", 1, u - 1)
                            leaf_products(DEPTH - 1, 0).then_inc(s_leafL, 1)
                        else:
                            leaf_products(DEPTH - 1, 1).then_inc(s_prob, 1)

        @block.scalar
        def _(act):
            seq = 0

            def chain(ins):
                nonlocal seq
                seq += 1
                ins.then_inc(s_aseq, 1)
                act.wait_ge(s_aseq, seq)

            def rstd(var, out_, done, done_sem):
                act.wait_ge(var, done)
                chain(nc.scalar.activation(out_[0][:, :], out_[1][:, :], ACT.Ln))
                nc.scalar.activation(out_[0][:, :], out_[0][:, :], ACT.Exp, scale=-0.5).then_inc(done_sem, 1)

            act.wait_ge(s_wfront, 16 * n_front)
            act.wait_ge(s_const, 1)
            nc.scalar.activation(c_silu[:, :], c_col[:, :], ACT.Silu).then_inc(s_csilu, 1)
            nc.scalar.preload_act_table_set("natural_log_exp_and_others")
            chain(nc.scalar.activation(knee_ln[:, :], zeros[:, 0:1], ACT.Exp, bias=neg_knee_col[:, :]))
            chain(nc.scalar.activation(knee_ln[:, :], knee_ln[:, :], ACT.Ln, bias=ones[:, 0:1]))
            act.wait_ge(s_w, 16 * n_rest)
            nc.scalar.activation(a_neg[:, :, :], alog[:, :, :], ACT.Exp).then_inc(s_aexp, 1)

            def softplus_parts(f, at):
                if at:
                    act.wait_ge(s_aseq, seq)
                if at == 0:
                    return nc.scalar.activation(sp_t[:, :, :], sp_abs[:, :, :], ACT.Relu,
                                                bias=neg_knee_col[:, :]), s_aseq
                if at == 1:
                    return nc.scalar.activation(sp_e[:, :, :], sp_t[:, :, :], ACT.Exp, scale=-1.0,
                                                bias=neg_knee_col[:, :]), s_aseq
                if at == 2:
                    return nc.scalar.activation(sp_t[:, :, :], sp_e[:, :, :], ACT.Square, scale=0.5,
                                                bias=neg_third_col[:, :]), s_poly
                if at == 3:
                    return nc.scalar.activation(sp_abs[:, :, :], sp_abs[:, :, :], ACT.Relu, scale=-1.0,
                                                bias=knee_col[:, :]), s_aseq
                if at == 4:
                    return nc.scalar.activation(sp_abs[:, :, :], sp_abs[:, :, :], ACT.Exp,
                                                bias=neg_knee_col[:, :]), s_aseq
                return nc.scalar.activation(sp_ln[:, :, :], sp_abs[:, :, :], ACT.Ln, bias=ones[:, 0:1]), s_sp

            for g in range(FIRST, LAST + 1):
                m2, f, t, u, late = g + 2, g + 1, g - 1, g - 2, g >= GROUPS
                norm, front, tail, leaf = m2 < GROUPS, 0 <= f < GROUPS, 0 <= t < GROUPS, 0 <= u < GROUPS
                fb, tb = f // CHUNKS, t // CHUNKS
                for s in range(STEPS):
                    k = g * STEPS + s
                    ke = k + AHEAD_EXP
                    if 0 <= ke < K:
                        ge, se = divmod(ke, STEPS)
                        n, half = divmod(se, HALVES)
                        if se < HALVES:
                            act.wait_ge(s_delta, HALVES * ge + half + 1)
                        if ke >= RD:
                            act.wait_ge(s_scan, ke - RD + 1)
                        if ke == 0:
                            act.wait_ge(s_aneg, 1)
                        nc.scalar.activation(dA[:, ke % RD, :], delta[:, ge % 2, half, :], ACT.Exp,
                                             scale=a_neg[:, half, n:n + 1]).then_inc(s_dA, 1)
                    if norm and s == N_STATS:
                        rstd(s_fvar, (f_rs, f_ve), m2 + 1, s_frs)
                    if norm and s == read_step("f", "tr", 0, False):
                        fb2 = m2 // CHUNKS
                        if m2:
                            wait_job(act, "f", "z", 1, m2 - 1)
                        if m2 % CHUNKS:
                            nc.scalar.activation(f_hT[:, 0:HALO], f_hT[:, T:T + HALO], ACT.Copy).then_inc(s_halo, 1)
                        else:
                            nc.scalar.activation(f_hT[:, 0:HALO], zeros[:, :], ACT.Copy).then_inc(s_halo, 1)
                        wait_job(act, "f", "tr", 0, m2)
                        if m2 == 0:
                            act.wait_ge(s_modc, 1)
                        act.wait_ge(s_halo, m2 + 1)
                        nc.scalar.activation(f_hT[:, HALO:HALO + T], job("f", "tr", 0, m2)[1][:, :], ACT.Identity,
                                             scale=mod_col[:, 1, fb2:fb2 + 1],
                                             bias=mod_col[:, 0, fb2:fb2 + 1]).then_inc(s_read["f", "act"], 1)
                    for half in range(HALVES):
                        if front and s == read_step("f", "xp", half, False):
                            wait_job(act, "f", "xp", half, f)
                            nc.scalar.activation(zu[:, f % 2, HALVES + half, :], job("f", "xp", half, f)[1][:, :],
                                                 ACT.Identity,
                                                 bias=cbias[:, half:half + 1]).then_inc(s_read["f", "act"], 1)
                        if front and s == read_step("f", "z", half, False):
                            wait_job(act, "f", "z", half, f)
                            if f >= 2:
                                act.wait_ge(s_gate, HALVES * (f - 2) + half + 1)
                            nc.scalar.activation(zu[:, f % 2, half, :], job("f", "z", half, f)[1][:, :],
                                                 ACT.Copy).then_inc(s_read["f", "act"], 1)
                    if front and s == F_SILU:
                        wait_read(act, "f", "z", 1, f)
                        nc.scalar.activation(zu[:, f % 2, :, :], zu[:, f % 2, :, :], ACT.Silu).then_inc(s_silu, 1)
                    if leaf and s == U_TANH[late]:
                        wait_read(act, "t", "node", 1, u)
                        nc.scalar.activation(go_r[:, :, :], go_r[:, :, :], ACT.Tanh, scale=0.5).then_inc(s_tanh, 1)
                    if front and s == F_SILU or leaf and s == U_TANH[late]:
                        nc.scalar.preload_act_table_set("natural_log_exp_and_others")
                    if leaf and s == U_SIG[late][0]:
                        act.wait_ge(s_tanh, u + 1)
                        chain(nc.scalar.activation(go_l[:, :, :], go_r[:, :, :], ACT.Identity, scale=-0.5,
                                                   bias=half_col[:, :]))
                    if leaf and s == U_SIG[late][1]:
                        nc.scalar.activation(go_r[:, :, :], go_r[:, :, :], ACT.Identity, scale=0.5,
                                             bias=half_col[:, :]).then_inc(s_sig, 1)
                    if front and s == read_step("f", "xd", 0, False):
                        wait_job(act, "f", "xd", 0, f)
                        if f:
                            act.wait_ge(s_cst, 16 * f)
                            act.wait_ge(s_r1, f)
                        nc.scalar.activation(xd[:, :], job("f", "xd", 0, f)[1][:, :],
                                             ACT.Copy).then_inc(s_read["f", "act"], 1)
                    if front and s == F_HI:
                        wait_read(act, "f", "xd", 0, f)
                        nc.scalar.activation(b_parts[:, f % 2, :], xd[:, :], ACT.Copy).then_inc(s_hi, 1)
                    if front and s == F_MID:
                        act.wait_ge(s_r1, f + 1)
                        nc.scalar.activation(b_parts[B_MID:P, f % 2, :], b_rest[B_MID:P, :],
                                             ACT.Copy).then_inc(s_mid, 1)
                    if front and s == F_LO:
                        act.wait_ge(s_r2, f + 1)
                        nc.scalar.activation(b_parts[B_LO:P, f % 2, :], b_rest[B_LO:P, :],
                                             ACT.Copy).then_inc(s_lo, 1)
                    if front and s in F_ABS:
                        half = F_ABS.index(s)
                        wait_job(act, "f", "dt", half, f)
                        bank = job("f", "dt", half, f)[1]
                        if f:
                            act.wait_ge(s_delta, HALVES * f)
                        nc.scalar.activation(delta[:, f % 2, half, :], bank[:, :], ACT.Relu,
                                             bias=dtb[:, half:half + 1])
                        nc.scalar.activation(sp_abs[:, half, :], bank[:, :], ACT.Abs,
                                             bias=dtb[:, half:half + 1]).then_inc(s_read["f", "act"], 1)
                    if front and s in F_SP:
                        at = F_SP.index(s)
                        if at == 0:
                            wait_read(act, "f", "dt", 1, f)
                        ins, done = softplus_parts(f, at)
                        seq += done is s_aseq
                        ins.then_inc(done, 1)
                    if tail and s == T_RSTD[late]:
                        rstd(s_tvar, (t_rs, t_ve), t + 1, s_trs)
                    for half in range(HALVES):
                        if tail and s == read_step("t", "yt", half, late):
                            wait_job(act, "t", "yt", half, t)
                            nc.scalar.activation(ygT[:, half, :], job("t", "yt", half, t)[1][:, :],
                                                 ACT.Copy).then_inc(s_read["t", "act"], 1)
                    if tail and s == read_step("t", "tr", 0, late):
                        wait_job(act, "t", "tr", 0, t)
                        nc.scalar.activation(t_hT[:, :], job("t", "tr", 0, t)[1][:, :], ACT.Identity,
                                             scale=mod_col[:, 4, tb:tb + 1],
                                             bias=mod_col[:, 3, tb:tb + 1]).then_inc(s_read["t", "act"], 1)
                    for part in range(2):
                        if leaf and s == read_step("t", "pt", part, late):
                            wait_job(act, "t", "pt", part, u)
                            if u and part == 0:
                                wait_job(act, "t", "ff", 0, u - 1)
                            nc.scalar.activation(probT[:, part, :], job("t", "pt", part, u)[1][:, :],
                                                 ACT.Copy).then_inc(s_read["t", "act"], 1)
                        if tail and s == read_step("t", "node", part, late):
                            wait_job(act, "t", "node", part, t)
                            if t:
                                act.wait_ge(s_prob, t)
                            nc.scalar.activation(go_r[:, 2 * part:2 * part + 2, :],
                                                 job("t", "node", part, t)[1][:, :].rearrange(
                                                     "p (i n) -> p i n", n=LEAVES),
                                                 ACT.Copy).then_inc(s_read["t", "act"], 1)

        @block.tensor
        def _(pe):
            def transpose(dst, src):
                return nc.tensor.transpose(dst, src, ident[:, :])

            pe.wait_ge(s_wfront, 16 * n_front)
            pe.wait_ge(s_const, 1)
            pe.wait_ge(s_csilu, 1)
            for m in range(6):
                last = nc.tensor.matmul(yb[0][:, m * BATCH:(m + 1) * BATCH], w_mod[:, m, :], c_silu[:, :],
                                        start=True, stop=True)
            last.then_inc(s_pre_pe, 1)
            pe.wait_ge(s_cwide, 1)
            for b in range(BATCH):
                for i, m in enumerate((2, 5)):
                    last = nc.tensor.matmul(yb[1][:, (2 * b + i) * DM:(2 * b + i + 1) * DM], c_wide[:, b, :],
                                            w_mod[:, m, :], start=True, stop=True)
            last.then_inc(s_pre_pe, 1)
            for hh in range(HALVES):
                last = nc.tensor.transpose(bb[0][0:R, hh * P:(hh + 1) * P], w_dtin[:, hh, :], ident[:, :])
            last.then_inc(s_wdtt, 1)
            pe.wait_ge(s_wdtc, 1)
            for hh in range(HALVES):
                last = nc.tensor.matmul(bb[1][:, hh * DI:(hh + 1) * DI], w_dtin_t[:, hh * P:(hh + 1) * P],
                                        w_dt[:, :], start=True, stop=True)
            last.then_inc(s_wdtp, 1)

            def weight_transposes():
                pe.wait_ge(s_w, 16 * n_rest)
                pe.wait_ge(s_wdt, 1)
                for i in range(2):
                    transpose(bb[0][:, i * P:(i + 1) * P], rout[:, i, :])
                    transpose(bb[1][:, i * P:(i + 1) * P], leafv[:, i, :])
                transpose(bb[2][:, 0:P], wo).then_inc(s_pre_pe, 1)

            def weight_products():
                pe.wait_ge(s_pre_cp, 1)
                nc.tensor.matmul(mb["t"][0][:, 0:2 * P], wq[:, :], rout_t[:, :], start=True, stop=True)
                for i in range(2):
                    last = nc.tensor.matmul(mb["t"][0][:, (2 + i) * DM:(3 + i) * DM],
                                            leafv_t[:, i * P:(i + 1) * P], wo_t[:, :], start=True, stop=True)
                last.then_inc(s_pre_pe, 1)

            def product(g, side, name, part, piece, pieces):
                n, bank = job(side, name, part, g)
                b = g // CHUNKS
                if piece == 0:
                    wait_bank(pe, side, n)
                tiles = range(piece * TILES // pieces, (piece + 1) * TILES // pieces)
                if (side, name) == ("f", "tr"):
                    pe.wait_ge(s_fxh, g + 1)
                    for i in tiles:
                        last = transpose(bank[:, i * P:(i + 1) * P], f_xhat[:, i, :])
                elif name == "xp":
                    if piece == 0:
                        wait_read(pe, "f", "tr", 0, g)
                        if g == 0:
                            pe.wait_ge(s_wconv, 1)
                    for tap in range(piece * TAPS // pieces, (piece + 1) * TAPS // pieces):
                        last = nc.tensor.matmul(bank[:, :], w_conv[:, tap, part * P:(part + 1) * P],
                                                f_hT[:, tap:tap + T], start=tap == 0, stop=tap == TAPS - 1)
                elif name == "z":
                    wait_read(pe, "f", "tr", 0, g)
                    for i in tiles:
                        last = nc.tensor.matmul(bank[:, i * P:(i + 1) * P],
                                                f_hT[:, HALO + i * P:HALO + (i + 1) * P],
                                                w_in[:, DI + part * P:DI + (part + 1) * P], start=True, stop=True)
                elif name == "xd":
                    if piece == 0:
                        pe.wait_ge(s_silu, g + 1)
                    last = nc.tensor.matmul(bank[:, :], w_xp[:, piece, :], zu[:, g % 2, HALVES + piece, :],
                                            start=piece == 0, stop=piece == HALVES - 1)
                elif name == "dt":
                    if piece == 0:
                        pe.wait_ge(s_silu, g + 1)
                        if g == 0:
                            pe.wait_ge(s_wdt, 1)
                    last = nc.tensor.matmul(bank[:, :], w_xdt[:, piece, part * P:(part + 1) * P],
                                            zu[:, g % 2, HALVES + piece, :],
                                            start=piece == 0, stop=piece == HALVES - 1)
                elif name == "yt":
                    pe.wait_ge(s_gate, HALVES * g + part + 1)
                    for i in tiles:
                        last = transpose(bank[:, i * P:(i + 1) * P], yg[:, part, i * P:(i + 1) * P])
                elif name == "out":
                    if piece == 0:
                        wait_read(pe, "t", "yt", 1, g)
                        if g == 0:
                            pe.wait_ge(s_wready, 1)
                    for i in tiles:
                        for hh in range(HALVES):
                            last = nc.tensor.matmul(bank[:, i * P:(i + 1) * P], ygT[:, hh, i * P:(i + 1) * P],
                                                    w_out_g[:, b, hh, :], start=hh == 0, stop=hh == HALVES - 1)
                elif (side, name) == ("t", "tr"):
                    pe.wait_ge(s_txh, g + 1)
                    for i in tiles:
                        last = transpose(bank[:, i * P:(i + 1) * P], t_xhat[:, i, :])
                elif name == "node":
                    wait_read(pe, "t", "tr", 0, g)
                    for i in range(2):
                        tile = 2 * part + i
                        last = nc.tensor.matmul(bank[:, i * LEAVES:(i + 1) * LEAVES],
                                                t_hT[:, tile * P:(tile + 1) * P], w_node[:, :],
                                                start=True, stop=True)
                elif name == "pt":
                    pe.wait_ge(s_prob, g + 1)
                    pe.wait_ge(s_leafL, g + 1)
                    for i in tiles:
                        last = transpose(bank[:, i * P:(i + 1) * P],
                                         prob[(DEPTH - 1) % 2][:, i, part * P:(part + 1) * P])
                else:
                    if piece == 0:
                        wait_read(pe, "t", "pt", 1, g)
                    for i in tiles:
                        dst = bank[:, i * P:(i + 1) * P]
                        nc.tensor.matmul(dst, ones[0:1, :], wo_b_g[0:1, b, :], start=True, stop=False)
                        for hh in range(2):
                            last = nc.tensor.matmul(dst, probT[:, hh, i * P:(i + 1) * P], leaf_out_g[:, b, hh, :],
                                                    start=False, stop=hh == 1)
                if piece == pieces - 1:
                    last.then_inc(s_job[side], 1)

            for g in range(FIRST, LAST + 1):
                for s in range(STEPS):
                    k = g * STEPS + s
                    kf, ks = k + AHEAD_FILL, k - LAG_SUM
                    if 0 <= kf < K and kf % HALVES == 0:
                        pair = kf // HALVES
                        gf, n = divmod(pair, N)
                        if n == 0:
                            pe.wait_ge(s_lo, gf + 1)
                        if pair == 0:
                            pe.wait_ge(s_pre_cp, 1)
                        if pair >= RB:
                            pe.wait_ge(s_dbu, pair - RB + 1)
                        nc.tensor.matmul(bb[pair % RB][:, :], sel[:, n, :], b_parts[:, gf % 2, :],
                                         start=True, stop=True).then_inc(s_fill, 1)
                    if 0 <= ks < K:
                        gs, ss = divmod(ks, STEPS)
                        n, half = divmod(ss, HALVES)
                        hg = HALVES * gs + half
                        bank = yb[hg % RY]
                        tiles = [slice(i * P, (i + 1) * P) for i in range(TILES)]
                        if n == 0:
                            if hg >= RY:
                                pe.wait_ge(s_gate, hg - RY + 1)
                            for tile in tiles:
                                nc.tensor.matmul(bank[:, tile], zu[:, gs % 2, HALVES + half, tile],
                                                 diag_d[:, half, :], start=tile.start == 0, stop=False,
                                                 skip_group_check=True)
                        pe.wait_ge(s_hc, ks // HALVES + 1)
                        for tile in tiles:
                            last = nc.tensor.matmul(bank[:, tile], h[:, ks // HALVES % RP, half, tile], ident[:, :],
                                                    start=False, stop=n == N - 1, is_transpose=True,
                                                    skip_group_check=True)
                        last.then_inc(s_sum, 1)
                    for side in JOBS:
                        for (name, part), (off, *by_phase) in JOBS[side].items():
                            steps = by_phase[g >= GROUPS]
                            if s in steps and 0 <= g + off < GROUPS:
                                product(g + off, side, name, part, steps.index(s), len(steps))
                    if g == -1 and s == 18:
                        weight_transposes()
                    if g == -1 and s == 20:
                        weight_products()

        @block.vector
        def _(dve):
            seq = 0

            def chain(ins):
                nonlocal seq
                seq += 1
                ins.then_inc(s_dseq, 1)
                dve.wait_ge(s_dseq, seq)

            v = nc.vector

            def stats(g, bn, mv, ve, ready):
                for i in range(TILES):
                    last = v.bn_stats(bn[:, i, :], xs[:, g * TILES + i, :])
                chain(last)
                for i in range(TILES):
                    last = v.bn_aggr(mv[:, i, :], bn[:, i, :])
                chain(last)
                v.tensor_scalar(ve[:, :], mv[:, :, 1], EPS, None, ALU.add).then_inc(ready, 1)

            def normalise(g, mv, rs, rs_ready, xhat, ready):
                dve.wait_ge(rs_ready, g + 1)
                for i in range(TILES):
                    last = v.tensor_scalar(xhat[:, i, :], xs[:, g * TILES + i, :], mv[:, i, 0:1], rs[:, i:i + 1],
                                           ALU.subtract, ALU.mult)
                last.then_inc(ready, 1)

            def front_weights():
                dve.wait_ge(s_csilu, 1)
                dve.wait_ge(s_const, 1)
                for b in range(BATCH):
                    last = v.tensor_scalar(c_wide[:, b, :], ones[:, :], c_silu[:, b:b + 1], None, ALU.mult)
                last.then_inc(s_cwide, 1)
                dve.wait_ge(s_wfront, 16 * n_front)
                for tap in range(TAPS):
                    last = v.tensor_tensor(w_conv[:, tap, :], w_in[:, 0:DI], taps[:, :, tap], ALU.mult)
                last.then_inc(s_wconv, 1)
                dve.wait_ge(s_pre_pe, 1)
                chain(v.tensor_copy(mod_col[:, :, :], yb[0][:, 0:6 * BATCH].rearrange("p (m b) -> p m b", b=BATCH)))
                v.tensor_scalar(mod_col[:, 1, :], mod_col[:, 1, :], 1.0, None, ALU.add)
                v.tensor_scalar(mod_col[:, 4, :], mod_col[:, 4, :], 1.0, None, ALU.add).then_inc(s_modc, 1)
                dve.wait_ge(s_wdtt, 1)
                v.tensor_copy(w_dtin_t[:, :], bb[0][0:R, 0:DI]).then_inc(s_wdtc, 1)
                dve.wait_ge(s_wdtp, 1)
                v.tensor_copy(w_xdt[:, :, :],
                              bb[1][:, 0:HALVES * DI].rearrange("p (h e) -> p h e", h=HALVES)).then_inc(s_wdt, 1)

            def gates():
                dve.wait_ge(s_pre_pe, 2)
                chain(v.tensor_copy(gate_raw[:, :, :, :],
                                    yb[1][:, :].rearrange("p (b i d) -> p b i d", b=BATCH, i=2)))
                v.tensor_scalar(gate_sgn[:, :, :, :], gate_raw[:, :, :, :], 0.0, 2.0, ALU.is_ge, ALU.mult)
                chain(v.scalar_tensor_tensor(gate_abs[:, :, :, :], gate_raw[:, :, :, :], -1.0,
                                             gate_raw[:, :, :, :], ALU.mult, ALU.max))
                chain(v.tensor_scalar(gate_abs[:, :, :, :], gate_abs[:, :, :, :], GATE_MIN, None, ALU.max))
                chain(v.scalar_tensor_tensor(gate_raw[:, :, :, :], gate_sgn[:, :, :, :], -1.0,
                                             gate_abs[:, :, :, :], ALU.add, ALU.mult))

            def scan_weights():
                dve.wait_ge(s_w, 16 * n_rest)
                for hh in range(HALVES):
                    v.tensor_scalar(diag_d[:, hh, :], ident[:, :], dskip[:, hh:hh + 1], None, ALU.mult)
                dve.wait_ge(s_aexp, 1)
                v.tensor_scalar(a_neg[:, :, :], a_neg[:, :, :], -1.0, None, ALU.mult).then_inc(s_aneg, 1)
                dve.wait_ge(s_pre_pe, 3)
                v.tensor_copy(rout_t[:, :], bb[0][:, 0:2 * P])
                v.tensor_copy(wo_t[:, :], bb[2][:, 0:P])
                v.tensor_copy(leafv_t[:, :], bb[1][:, 0:2 * P]).then_inc(s_pre_cp, 1)

            def tail_weights():
                dve.wait_ge(s_pre_pe, 4)
                v.tensor_copy(w_node[:, :], mb["t"][0][:, 0:2 * P])
                chain(v.tensor_copy(leaf_out[:, :, :],
                                    mb["t"][0][:, 2 * DM:4 * DM].rearrange("p (i d) -> p i d", d=DM)))
                for b in range(BATCH):
                    for i in range(2):
                        v.tensor_tensor(w_out_g[:, b, i, :], w_out[:, i, :], gate_raw[:, b, 0, :], ALU.mult)
                        v.tensor_tensor(leaf_out_g[:, b, i, :], leaf_out[:, i, :], gate_raw[:, b, 1, :], ALU.mult)
                    last = v.tensor_tensor(wo_b_g[0:1, b, :], wo_b[0:1, :], gate_raw[0:1, b, 1, :], ALU.mult)
                last.then_inc(s_wready, 1)

            for g in range(FIRST, LAST + 1):
                m2, f, t, u, late = g + 2, g + 1, g - 1, g - 2, g >= GROUPS
                norm, front, tail, leaf = m2 < GROUPS, 0 <= f < GROUPS, 0 <= t < GROUPS, 0 <= u < GROUPS
                for s in range(STEPS):
                    if g == FIRST and s == N_XHAT:
                        front_weights()
                    if g == -1 and s == 12:
                        gates()
                    if g == -1 and s == 20:
                        scan_weights()
                    if g == -1 and s == 29:
                        tail_weights()
                    k = g * STEPS + s
                    if 0 <= k < K:
                        n, half = divmod(s, HALVES)
                        pair = k // HALVES
                        dve.wait_ge(s_dA, k + 1)
                        if half == 0:
                            dve.wait_ge(s_dbu, pair + 1)
                            if pair >= RP:
                                dve.wait_ge(s_sum, HALVES * (pair - RP + 1))
                            if g % CHUNKS:
                                dve.wait_ge(s_save, saves(pair - N) + 1)
                        start = state[:, n, half:half + 1] if g % CHUNKS else 0.0
                        v.tensor_tensor_scan(h[:, pair % RP, half, :], dA[:, k % RD, :], dbu[:, pair % RW, half, :],
                                             start, ALU.mult, ALU.add).then_inc(s_scan, 1)
                        if half == 0 and pair and saved(pair - 1):
                            dve.wait_ge(s_scan, k)
                            v.tensor_copy(state[:, (pair - 1) % N, :],
                                          h[:, (pair - 1) % RP, :, T - 1]).then_inc(s_save, 1)
                    kd = k + AHEAD_DBU
                    if 0 <= kd < K and kd % HALVES == 0:
                        pair = kd // HALVES
                        gd, n = divmod(pair, N)
                        if n == 0:
                            dve.wait_ge(s_du, HALVES * (gd + 1))
                        dve.wait_ge(s_fill, pair + 1)
                        if pair >= RW:
                            dve.wait_ge(s_scan, HALVES * (pair - RW + 1))
                        v.tensor_tensor(dbu[:, pair % RW, :, :], du[:, gd % 2, :, :],
                                        bb[pair % RB][:, :].unsqueeze(1).broadcast_to([P, HALVES, T]),
                                        ALU.mult).then_inc(s_dbu, 1)
                    if norm and s == N_STATS:
                        if m2 == 0:
                            dve.wait_ge(s_x0, 16)
                        else:
                            dve.wait_ge(s_x, 16 * (GROUPS - 1))
                        stats(m2, f_bn, f_mv, f_ve, s_fvar)
                    if norm and s == N_XHAT:
                        if m2:
                            wait_job(dve, "f", "tr", 0, m2 - 1)
                        normalise(m2, f_mv, f_rs, s_frs, f_xhat, s_fxh)
                    if front and s in F_POLY:
                        at = F_POLY.index(s)
                        if at == 0:
                            dve.wait_ge(s_poly, f + 1)
                        else:
                            dve.wait_ge(s_dseq, poly_seq)
                        if at < 2:
                            last = v.scalar_tensor_tensor(sp_t[:, :, :], sp_t[:, :, :], (7.0 / 18.0, -1.0)[at],
                                                          sp_e[:, :, :], ALU.add, ALU.mult)
                        else:
                            dve.wait_ge(s_sp, f + 1)
                            last = v.scalar_tensor_tensor(sp_ln[:, :, :], sp_ln[:, :, :], knee_ln[:, :],
                                                          sp_t[:, :, :], ALU.subtract, ALU.subtract)
                        seq += 1
                        last.then_inc(s_dseq, 1)
                        poly_seq = seq
                    if front and s == F_DELTA:
                        dve.wait_ge(s_dseq, poly_seq)
                        for half in range(HALVES):
                            v.tensor_tensor(delta[:, f % 2, half, :], delta[:, f % 2, half, :], sp_ln[:, half, :],
                                            ALU.add).then_inc(s_delta, 1)
                    if tail and s in T_GATE[late]:
                        half = T_GATE[late].index(s)
                        hg = HALVES * t + half
                        dve.wait_ge(s_sum, t * STEPS + STEPS - HALVES + half + 1)
                        if t:
                            wait_job(dve, "t", "yt", half, t - 1)
                        v.tensor_tensor(yg[:, half, :], yb[hg % RY][:, :], zu[:, t % 2, half, :],
                                        ALU.mult).then_inc(s_gate, 1)
                    if tail and s == T_ADD[late]:
                        wait_job(dve, "t", "out", 0, t)
                        x1 = xs[:, t * TILES:(t + 1) * TILES, :]
                        v.tensor_tensor(x1, job("t", "out", 0, t)[1][:, :].rearrange("p (i d) -> p i d", d=DM), x1,
                                        ALU.add).then_inc(s_read["t", "dve"], 1)
                    if tail and s == T_STATS[late]:
                        wait_read(dve, "t", "out", 0, t)
                        stats(t, t_bn, t_mv, t_ve, s_tvar)
                    if tail and s == T_XHAT[late]:
                        if t:
                            wait_job(dve, "t", "tr", 0, t - 1)
                        normalise(t, t_mv, t_rs, s_trs, t_xhat, s_txh)
                    if leaf and s == U_FIN[late]:
                        wait_job(dve, "t", "ff", 0, u)
                        x1 = xs[:, u * TILES:(u + 1) * TILES, :]
                        v.tensor_tensor(x1, job("t", "ff", 0, u)[1][:, :].rearrange("p (i d) -> p i d", d=DM), x1,
                                        ALU.add).then_inc(s_read["t", "dve"], 1)


_INS = ["L0_attn_x", "L0_attn_W_in", "L0_attn_conv_w", "L0_attn_conv_b", "L0_attn_W_xp", "L0_attn_W_dt",
        "L0_attn_dt_bias", "L0_attn_A_log", "L0_attn_D_skip", "L0_attn_W_out", "L0_ffn_Wq", "L0_ffn_routers",
        "L0_ffn_leaf_values", "L0_ffn_Wout_w", "L0_ffn_Wout_b", "L0_c", "L0_wmod"]
_OUTS = [((2, 2048, 128), "float32")]


def kernel(**inputs):
    import numpy as _np
    import concourse.bacc as _bacc
    from concourse import mybir as _mybir
    from concourse.bass_utils import run_bass_kernel_spmd as _run

    nc = _bacc.Bacc("TRN2", target_bir_lowering=False, num_devices=1)
    arrays, args = {}, []
    for name in _INS:
        a = _np.ascontiguousarray(inputs[name])
        arrays[f"in_{name}_dram"] = a
        args.append(nc.dram_tensor(f"in_{name}_dram", a.shape, _mybir.dt.from_np(a.dtype), kind="ExternalInput").ap())
    for i, (shape, dtype) in enumerate(_OUTS):
        dt = _mybir.dt.from_np(_np.dtype(dtype))
        args.append(nc.dram_tensor(f"out_{i}_dram", shape, dt, kind="ExternalOutput").ap())
    bass_adaln_mamba_tree_ffn_kernel(nc, *args)
    r = _run(nc, [arrays], core_ids=[0])
    got = tuple(r.results[0][f"out_{i}_dram"] for i in range(len(_OUTS)))
    return got[0]
```

```python
import math

import concourse.bass as bass
from concourse import mybir
from contextlib import ExitStack


def bass_adaln_mamba_tree_ffn_kernel(
    nc: bass.Bass,
    x: bass.AP,
    W_in: bass.AP,
    conv_w: bass.AP,
    conv_b: bass.AP,
    W_xp: bass.AP,
    W_dt: bass.AP,
    dt_bias: bass.AP,
    A_log: bass.AP,
    D_skip: bass.AP,
    W_out: bass.AP,
    Wq: bass.AP,
    routers: bass.AP,
    leaf_values: bass.AP,
    Wo: bass.AP,
    Wo_b: bass.AP,
    c: bass.AP,
    wmod: bass.AP,
    out: bass.AP,
):
    f32 = mybir.dt.float32
    bf16 = mybir.dt.bfloat16
    ALU = mybir.AluOpType
    ACT = mybir.ActivationFunctionType

    P = 128
    BATCH, L, DM = x.shape
    DI = W_out.shape[0]
    HALVES = DI // P
    R = W_dt.shape[0]
    N = (W_xp.shape[1] - R) // 2
    TAPS = conv_w.shape[2]
    HALO = TAPS - 1
    T = 512
    TILES = T // P
    CHUNKS = L // T
    GROUPS = BATCH * CHUNKS
    STEPS = N * HALVES
    K = GROUPS * STEPS
    NODES = routers.shape[0]
    LEAVES = leaf_values.shape[0]
    DEPTH = LEAVES.bit_length() - 1
    EPS = 1e-5
    THETA = 2.0 ** -5
    LOG_KNEE = math.log1p(THETA)
    GATE_MIN = 0.25
    QUARTERS = 4
    NQ = N // QUARTERS
    B_HI, C_ROW, B_MID, B_LO = 0, N, 64, 96

    PAIRS = K // HALVES
    RB, RY, RD, RP, RW = 3, HALVES, 6, 5, 2
    RM = {"f": 2, "t": 1}
    AHEAD_EXP, AHEAD_FILL, AHEAD_DBU, LAG_SUM = 5, 5, 2, 5

    N_STATS = {g: 10 if g == -1 else 5 for g in range(-2, GROUPS)}
    N_XHAT = {g: N_STATS[g] + 2 for g in N_STATS}
    F_SILU_0 = 5
    F_SILU, F_ABS, F_SP, F_POLY, F_DELTA, F_DU = 10, (13, 15), (16, 17, 18, 20), (20, 21, 23), 24, (25, 26)
    F_HI, F_R1, F_MID, F_R2, F_LO = 21, 22, 23, 24, 25
    T_GATE, T_ADD, T_STATS, T_RSTD, T_XHAT = ((4, 5), (4, 5)), (14, 11), (15, 12), (15, 13), (18, 14)
    U_TANH, U_SIG, U_LEAF = (F_SILU, 0), (11, 1), ((13, 14, 15, 16, 17, 18), (2, 3, 4, 5, 6, 7))
    U_FIN = (28, 22)

    JOBS = {
        "f": {("xp", 0): (1, (0, 1), ()), ("xp", 1): (1, (3, 4), ()), ("z", 0): (1, (7,), ()),
              ("z", 1): (1, (8,), ()), ("dt", 0): (1, (11, 12), ()), ("dt", 1): (1, (13, 14), ()),
              ("xd", 0): (1, (15, 16), ()), ("tr", 0): (2, (28,), ())},
        "t": {("yt", 0): (-1, (6,), (6,)), ("yt", 1): (-1, (8,), (8,)), ("out", 0): (-1, (10, 11), (10,)),
              ("tr", 0): (-1, (19,), (15,)), ("pt", 0): (-2, (21,), (13,)), ("pt", 1): (-2, (23,), (14,)),
              ("ff", 0): (-2, (25, 26), (21,)), ("node", 0): (-1, (28,), (17,)),
              ("node", 1): (-1, (30,), (19,))},
    }
    BY_DVE = {"out", "ff"}
    WARM_START = 9
    WARM = {(-1, 18): 8, (-1, 19): 3, (-1, 21): 3}
    WARM.update({(GROUPS, s): 1 for s in range(6, 26)})
    WARM.update({(GROUPS, 12): 9, (GROUPS, 15): 4, (GROUPS, 17): 4, (GROUPS + 1, 12): 24})
    FIRST, LAST = -2, GROUPS + 1
    job_at, read_at, reads = {}, {"f": [], "t": []}, {}
    for side in JOBS:
        for g in range(FIRST, LAST + 1):
            for (name, part), (off, *steps) in sorted(JOBS[side].items(), key=lambda job: job[1][1 + (g >= GROUPS)]):
                if 0 <= g + off < GROUPS:
                    job_at[side, name, part, g + off] = len(read_at[side])
                    by = "dve" if name in BY_DVE else "act"
                    reads[side, by] = reads.get((side, by), 0) + 1
                    read_at[side].append((side, by, reads[side, by]))

    ctx = ExitStack()
    with ctx:
        def sb(name, shape, dt=f32):
            return ctx.enter_context(nc.sbuf_tensor(name, shape, dt))

        def sem(name):
            return ctx.enter_context(nc.semaphore(name))

        ident = sb("ident", [P, P])
        sel = sb("sel", [P, N, P], bf16)
        ones = sb("ones", [P, P])
        idle = sb("idle", [P, T], bf16)
        neg_ident = sb("neg_ident", [P, P], bf16)
        half_col = sb("half_col", [P, 1])
        neg_third_col = sb("neg_third_col", [P, 1])
        neg_log_knee = sb("neg_log_knee", [P, 1])
        w_in = sb("w_in", [P, 2 * DI])
        w_xp = sb("w_xp", [P, HALVES, P])
        w_dt = sb("w_dt", [R, DI])
        dtb = sb("dtb", [P, HALVES])
        w_xdt = sb("w_xdt", [P, HALVES, DI])
        w_out = sb("w_out", [P, HALVES, DM])
        wq = sb("wq", [P, DM])
        wo_b = sb("wo_b", [1, DM])
        w_conv = sb("w_conv", [P, TAPS, DI])
        zeros = sb("zeros", [P, HALO])
        cbias = sb("cbias", [P, HALVES])
        dskip = sb("dskip", [P, HALVES])
        alog = sb("alog", [P, HALVES, N])
        a_neg = sb("a_neg", [P, HALVES, N])
        c_col = sb("c_col", [P, BATCH])
        c_silu = sb("c_silu", [P, BATCH])
        c_wide = sb("c_wide", [P, BATCH, P])
        mod_col = sb("mod_col", [P, 6, BATCH])
        rout_t = sb("rout_t", [P, 2 * P])
        leafv_t = sb("leafv_t", [P, 2 * P])
        wo_t = sb("wo_t", [P, DM])
        w_node = sb("w_node", [P, 2 * P])
        leaf_out = sb("leaf_out", [P, 2, DM])
        w_out_g = sb("w_out_g", [P, BATCH, HALVES, DM])
        leaf_out_g = sb("leaf_out_g", [P, BATCH, 2, DM])
        wo_b_g = sb("wo_b_g", [1, BATCH, DM])
        diag_d = sb("diag_d", [P, HALVES, P])
        xs = sb("xs", [P, GROUPS * TILES, DM])
        dA = sb("dA", [P, RD, T])
        dbu = sb("dbu", [P, RW, HALVES, T])
        h = sb("h", [P, RP, HALVES, T])
        state = sb("state", [P, N, HALVES])
        c_rows = sb("c_rows", [P, QUARTERS, NQ, T])
        zu = sb("zu", [P, 2, 2 * HALVES, T])
        delta = sb("delta", [P, 2, HALVES, T])
        du = sb("du", [P, 2, HALVES, T])
        b_parts = sb("b_parts", [P, 2, T], bf16)
        f_bn = sb("f_bn", [P, TILES, 6])
        f_mv = sb("f_mv", [P, TILES, 2])
        f_ve = sb("f_ve", [P, TILES])
        f_rs = sb("f_rs", [P, TILES])
        f_xhat = sb("f_xhat", [P, TILES, DM])
        f_hT = sb("f_hT", [P, HALO + T])
        xd = sb("xd", [P, T])
        sp_abs = sb("sp_abs", [P, HALVES, T])
        sp_e = sb("sp_e", [P, HALVES, T])
        sp_t = sb("sp_t", [P, HALVES, T])
        sp_ln = sb("sp_ln", [P, HALVES, T])
        yg = sb("yg", [P, HALVES, T])
        ygT = sb("ygT", [P, HALVES, T])
        t_bn = sb("t_bn", [P, TILES, 6])
        t_mv = sb("t_mv", [P, TILES, 2])
        t_ve = sb("t_ve", [P, TILES])
        t_rs = sb("t_rs", [P, TILES])
        t_xhat = sb("t_xhat", [P, TILES, DM])
        t_hT = sb("t_hT", [P, T])
        go_r = sb("go_r", [P, TILES, LEAVES])
        prob = [sb("prob_even", [P, TILES, LEAVES // 2]), sb("prob_odd", [P, TILES, LEAVES])]
        probT = sb("probT", [P, 2, T])
        taps = ygT[:, :, :].rearrange("p a (b k) -> p (a b) k", k=TAPS)
        rout = yg[:, 0, 0:2 * DM].rearrange("p (i d) -> p i d", i=2)
        leafv = yg[:, 0, 2 * DM:4 * DM].rearrange("p (i d) -> p i d", i=2)
        wo = yg[:, 1, 0:DM]
        w_dtin = yg[:, 1, DM:DM + HALVES * R].rearrange("p (h r) -> p h r", h=HALVES)
        w_dtin_t = t_xhat[0:R, 0:HALVES, :].rearrange("r h e -> r (h e)")
        w_mod = probT[:, :, :].rearrange("p a t -> p (a t)")[:, 0:6 * DM].rearrange("p (j d) -> p j d", j=6)
        gate_raw = prob[0][:, :, :].rearrange("p i n -> p (i n)").rearrange("p (b i d) -> p b i d", b=BATCH, i=2)
        gate_sgn = prob[1][:, 0:BATCH, :].rearrange("p b (i d) -> p b i d", i=2)
        gate_abs = prob[1][:, BATCH:2 * BATCH, :].rearrange("p b (i d) -> p b i d", i=2)

        bb = [ctx.enter_context(nc.psum_tensor(f"bb{i}", [P, T], f32)) for i in range(RB)]
        yb = [ctx.enter_context(nc.psum_tensor(f"yb{i}", [P, T], f32)) for i in range(RY)]
        mb = {side: [ctx.enter_context(nc.psum_tensor(f"m{side}{i}", [P, T], f32)) for i in range(RM[side])]
              for side in RM}
        c_dram = nc.dram_tensor("c_dram", [GROUPS, N, T], f32, kind="Internal").ap()

        s_w = sem("weights_loaded")
        s_x0 = sem("x_of_group_0_loaded")
        s_x = sem("x_of_other_groups_loaded")
        s_rt = sem("rout_zeroed")
        s_wz = sem("w_xp_zeroed")
        s_idle = sem("idle_operand_made")
        s_const = sem("constants_made")
        s_pool = sem("pool_seq")
        s_dseq = sem("dve_seq")
        s_aseq = sem("act_seq")
        s_pre_pe = sem("pre_products")
        s_pre_cp = sem("pre_copied")
        s_csilu = sem("c_silu_ready")
        s_cwide = sem("c_wide_ready")
        s_aexp = sem("a_exp_ready")
        s_aneg = sem("a_neg_ready")
        s_wready = sem("scaled_weights_ready")
        s_fill = sem("b_filled")
        s_dbu = sem("dbu_done")
        s_dA = sem("dA_done")
        s_scan = sem("scan_done")
        s_save = sem("state_saved")
        s_hc = sem("hc_done")
        s_sum = sem("sum_done")
        s_job = {"f": sem("f_product_done"), "t": sem("t_product_done")}
        s_read = {("f", "act"): sem("f_product_read_by_act"), ("t", "act"): sem("t_product_read_by_act"),
                  ("t", "dve"): sem("t_product_read_by_dve")}
        s_halo = sem("halo_ready")
        s_wmod = sem("modulation_weights_loaded")
        s_wcv = sem("conv_weights_loaded")
        s_wfront = sem("front_weights_loaded")
        s_wconv = sem("conv_weights_ready")
        s_wdtt = sem("dt_weights_transposed")
        s_wdtc = sem("dt_weights_copied")
        s_wdtp = sem("dt_weights_multiplied")
        s_wdt = sem("dt_weights_ready")
        s_modc = sem("mod_columns_ready")
        s_fvar = sem("f_var_ready")
        s_frs = sem("f_rstd_ready")
        s_fxh = sem("f_xhat_ready")
        s_silu = sem("u_silu_done")
        s_zsilu = sem("z_silu_done")
        s_hi = sem("b_hi_ready")
        s_r1 = sem("b_rest1_ready")
        s_mid = sem("b_mid_ready")
        s_r2 = sem("b_rest2_ready")
        s_lo = sem("b_parts_ready")
        s_poly = sem("softplus_series_ready")
        s_sp = sem("softplus_ln_ready")
        s_delta = sem("delta_ready")
        s_du = sem("du_ready")
        s_cst = sem("c_stored")
        s_cld = [sem(f"c_loaded{q}") for q in range(QUARTERS)]
        s_gate = sem("y_gated")
        s_tvar = sem("t_var_ready")
        s_trs = sem("t_rstd_ready")
        s_txh = sem("t_xhat_ready")
        s_tanh = sem("node_tanh_ready")
        s_sig = sem("node_sigmoids_ready")
        s_prob = sem("leaf_probs_ready")
        s_out = sem("out_stored")

        block = ctx.enter_context(nc.Block())

        def job(side, name, part, g):
            n = job_at[side, name, part, g]
            return n, mb[side][n % RM[side]]

        def read_step(side, name, part, late):
            return JOBS[side][name, part][1 + late][-1] + 1

        def wait_job(eng, side, name, part, g):
            eng.wait_ge(s_job[side], job_at[side, name, part, g] + 1)

        def wait_read(eng, side, name, part, g):
            _, by, count = read_at[side][job_at[side, name, part, g]]
            eng.wait_ge(s_read[side, by], count)

        def wait_bank(eng, side, n):
            if n >= RM[side]:
                _, by, count = read_at[side][n - RM[side]]
                eng.wait_ge(s_read[side, by], count)

        def saves(pair):
            g, n = divmod(pair, N)
            return (g // CHUNKS) * (CHUNKS - 1) * N + (g % CHUNKS) * N + (n if saved(pair) else 0)

        def saved(pair):
            return pair // N % CHUNKS < CHUNKS - 1

        n_mod, n_conv, n_front, n_rest = 2, 3, 7, 9

        def leaf_products(eng, level, side):
            n = 1 << level
            child = prob[level % 2][:, :, 0:2 * n].rearrange("p i (n two) -> p i n two", two=2)
            node = go_r[:, :, n - 1:2 * n - 1]
            parent = prob[(level + 1) % 2][:, :, 0:n] if level else ones[:, 0:TILES].unsqueeze(2)
            if side:
                return eng.tensor_tensor(child[:, :, :, 1], parent, node, ALU.mult)
            return eng.tensor_tensor(child[:, :, :, 0], parent, child[:, :, :, 1], ALU.subtract)

        @block.sync
        def _(sp):
            count = {s_wmod: 0, s_wcv: 0, s_wfront: 0, s_w: 0}

            def load(dst, src, which=s_w):
                count[which] += 1
                sp.dma_start(dst, src, allow_slow_non_contiguous=True).then_inc(which, 16)

            def load_x(g):
                b, ch = divmod(g, CHUNKS)
                sp.dma_start(xs[:, g * TILES:(g + 1) * TILES, :],
                             x[b, ch * T:(ch + 1) * T, :].rearrange("(i p) d -> p i d", p=P)).then_inc(s_x if g else s_x0, 16)

            load_x(0)
            load(c_col[:, :], c.rearrange("b k -> k b"), s_wmod)
            load(w_mod[:, :, :], wmod.rearrange("k (j d) -> k j d", j=6), s_wmod)
            load(w_in[:, :], W_in, s_wcv)
            load(taps[:, :, :].rearrange("p e k -> p (e k)"),
                 conv_w.rearrange("e o k -> (e o k)").partition_broadcast(P), s_wcv)
            load(cbias[:, :], conv_b.rearrange("(h p) -> p h", p=P), s_wcv)
            sp.wait_ge(s_wz, 1)
            xp_v = W_xp.rearrange("(h p) j -> p h j", p=P)
            for row, first, width in ((B_HI, R, N), (C_ROW, R + N, N), (B_MID, R, N), (B_LO, R, N)):
                load(w_xp[:, :, row:row + width], xp_v[:, :, first:first + width], s_wfront)
            load(w_dt[:, :], W_dt, s_wfront)
            load(dtb[:, :], dt_bias.rearrange("(h p) -> p h", p=P), s_wfront)
            load(w_dtin[:, :, :], xp_v[:, :, 0:R], s_wfront)
            load(alog[:, :, :], A_log.rearrange("(h p) n -> p h n", p=P))
            load(dskip[:, :], D_skip.rearrange("(h p) -> p h", p=P))
            load(w_out[:, :, :], W_out.rearrange("(h p) d -> p h d", p=P))
            load(wq[:, :], Wq)
            load(leafv[:, :, :], leaf_values.rearrange("(h p) d -> p h d", p=P))
            load(wo, Wo)
            load(wo_b[:, :], Wo_b.rearrange("(a n) -> a n", a=1))
            sp.wait_ge(s_rt, 1)
            load(rout[:, 0, :], routers[0:P, :])
            load(rout[0:NODES - P, 1, :], routers[P:NODES, :])
            assert list(count.values()) == [n_mod, n_conv, n_front, n_rest]
            for g in range(1, GROUPS):
                load_x(g)

            for g in range(-1, LAST + 1):
                f, u = g + 1, g - 2
                if f < GROUPS:
                    wait_read(sp, "f", "xd", 0, f)
                    sp.dma_start(c_dram[f, :, :], xd[C_ROW:C_ROW + N, :]).then_inc(s_cst, 16)
                    sp.wait_ge(s_cst, 16 * (f + 1))
                    for q in range(QUARTERS):
                        if g >= 0:
                            sp.wait_ge(s_hc, g * N + (q + 1) * NQ)
                        src = c_dram[f, q * NQ:(q + 1) * NQ, :].rearrange("n t -> (n t)")
                        sp.dma_start(c_rows[:, q, :, :].rearrange("p n t -> p (n t)"),
                                     src.partition_broadcast(P)).then_inc(s_cld[q], 16)
                if u >= 0:
                    b, ch = divmod(u, CHUNKS)
                    wait_read(sp, "t", "ff", 0, u)
                    sp.dma_start(out[b, ch * T:(ch + 1) * T, :].rearrange("(i p) d -> p i d", p=P),
                                 xs[:, u * TILES:(u + 1) * TILES, :]).then_inc(s_out, 16)
            sp.wait_ge(s_out, 16 * GROUPS)

        @block.gpsimd
        def _(pool):
            seq = 0

            def chain(ins):
                nonlocal seq
                seq += 1
                ins.then_inc(s_pool, 1)
                pool.wait_ge(s_pool, seq)

            nc.gpsimd.memset(idle[:, :], 1.0).then_inc(s_idle, 1)
            nc.gpsimd.memset(w_xp[:, :, :], 0.0).then_inc(s_wz, 1)
            nc.gpsimd.memset(rout[:, 1, :], 0.0).then_inc(s_rt, 1)
            chain(nc.gpsimd.memset(ident[:, :], 0.0))
            chain(nc.gpsimd.affine_select(out=ident[:, :], in_=ident[:, :], compare_op=ALU.not_equal, fill=1.0,
                                          base=0, pattern=[[-1, P]], channel_multiplier=1))
            nc.gpsimd.memset(half_col[:, :], 0.5)
            nc.gpsimd.memset(neg_third_col[:, :], -1.0 / 3.0)
            nc.gpsimd.memset(neg_log_knee[:, :], -LOG_KNEE)
            chain(nc.gpsimd.memset(ones[:, :], 1.0))
            nc.gpsimd.memset(zeros[:, :], 0.0).then_inc(s_const, 1)
            chain(nc.gpsimd.memset(sel[:, :, :], 0.0))
            for first in (B_HI, B_MID, B_LO):
                chain(nc.gpsimd.affine_select(out=sel[:, :, :], in_=sel[:, :, :], compare_op=ALU.not_equal,
                                              fill=1.0, base=-first, pattern=[[-1, N], [0, P]],
                                              channel_multiplier=1))
            chain(nc.gpsimd.memset(neg_ident[:, :], 0.0))
            nc.gpsimd.affine_select(out=neg_ident[:, :], in_=neg_ident[:, :], compare_op=ALU.not_equal, fill=-1.0,
                                    base=0, pattern=[[-1, P]], channel_multiplier=1).then_inc(s_const, 1)

            for g in range(-1, LAST + 1):
                f, u, late = g + 1, g - 2, g >= GROUPS
                front, leaf = f < GROUPS, 0 <= u < GROUPS
                for s in range(STEPS):
                    if 0 <= g < GROUPS and s % HALVES == HALVES - 1:
                        n = s // HALVES
                        pair, q = g * N + n, n // NQ
                        if n % NQ == 0:
                            pool.wait_ge(s_cld[q], 16 * (g + 1))
                        pool.wait_ge(s_scan, HALVES * (pair + 1))
                        if saved(pair):
                            pool.wait_ge(s_save, saves(pair) + 1)
                        hp = h[:, pair % RP, :, :]
                        nc.gpsimd.tensor_tensor(hp, hp, c_rows[:, q, n % NQ, :].unsqueeze(1).broadcast_to([P, HALVES, T]),
                                                ALU.mult).then_inc(s_hc, 1)
                    if front and s in F_DU:
                        half = F_DU.index(s)
                        pool.wait_ge(s_delta, HALVES * f + half + 1)
                        pool.wait_ge(s_silu, f + 1)
                        nc.gpsimd.tensor_tensor(du[:, f % 2, half, :], delta[:, f % 2, half, :],
                                                zu[:, f % 2, HALVES + half, :], ALU.mult).then_inc(s_du, 1)
                    if leaf and u < GROUPS - 1 and s in U_LEAF[late]:
                        at = U_LEAF[late].index(s)
                        if at == 0:
                            pool.wait_ge(s_sig, u + 1)
                            for level in range(DEPTH - 4):
                                chain(leaf_products(nc.gpsimd, level, 1))
                                chain(leaf_products(nc.gpsimd, level, 0))
                        elif at < 4:
                            chain(leaf_products(nc.gpsimd, DEPTH - 5 + at, 1))
                            chain(leaf_products(nc.gpsimd, DEPTH - 5 + at, 0))
                        elif at == 4:
                            if u:
                                wait_job(pool, "t", "pt", 1, u - 1)
                            chain(leaf_products(nc.gpsimd, DEPTH - 1, 1))
                        else:
                            leaf_products(nc.gpsimd, DEPTH - 1, 0).then_inc(s_prob, 1)

        @block.scalar
        def _(act):
            seq = 0

            def chain(ins):
                nonlocal seq
                seq += 1
                ins.then_inc(s_aseq, 1)
                act.wait_ge(s_aseq, seq)

            def rstd(var, out_, done, done_sem):
                act.wait_ge(var, done)
                chain(nc.scalar.activation(out_[0][:, :], out_[1][:, :], ACT.Ln))
                nc.scalar.activation(out_[0][:, :], out_[0][:, :], ACT.Exp, scale=-0.5).then_inc(done_sem, 1)

            act.wait_ge(s_wmod, 16 * n_mod)
            nc.scalar.activation(c_silu[:, :], c_col[:, :], ACT.Silu).then_inc(s_csilu, 1)
            nc.scalar.preload_act_table_set("natural_log_exp_and_others")

            def softplus_parts(f, at):
                if at == 0:
                    return nc.scalar.activation(sp_e[:, :, :], sp_abs[:, :, :], ACT.Exp, scale=-1.0), s_aseq
                act.wait_ge(s_aseq, seq)
                if at == 1:
                    return nc.scalar.activation(sp_t[:, :, :], sp_e[:, :, :], ACT.Square, scale=0.5,
                                                bias=neg_third_col[:, :]), s_poly
                if at == 2:
                    return nc.scalar.activation(sp_ln[:, :, :], sp_e[:, :, :], ACT.Ln, bias=ones[:, 0:1]), s_aseq
                return nc.scalar.activation(sp_ln[:, :, :], sp_ln[:, :, :], ACT.Relu,
                                            bias=neg_log_knee[:, :]), s_sp

            for g in range(FIRST, LAST + 1):
                m2, f, t, u, late = g + 2, g + 1, g - 1, g - 2, g >= GROUPS
                norm, front, tail, leaf = m2 < GROUPS, 0 <= f < GROUPS, 0 <= t < GROUPS, 0 <= u < GROUPS
                fb, tb = f // CHUNKS, t // CHUNKS
                for s in range(STEPS):
                    k = g * STEPS + s
                    ke = k + AHEAD_EXP
                    if 0 <= ke < K:
                        ge, se = divmod(ke, STEPS)
                        n, half = divmod(se, HALVES)
                        if se < HALVES:
                            act.wait_ge(s_delta, HALVES * ge + half + 1)
                        if ke >= RD:
                            act.wait_ge(s_scan, ke - RD + 1)
                        if ke == 0:
                            act.wait_ge(s_aneg, 1)
                        nc.scalar.activation(dA[:, ke % RD, :], delta[:, ge % 2, half, :], ACT.Exp,
                                             scale=a_neg[:, half, n:n + 1]).then_inc(s_dA, 1)
                    if g == -1 and s == 11:
                        act.wait_ge(s_wfront, 16 * n_front)
                        act.wait_ge(s_w, 16 * n_rest)
                        act.wait_ge(s_const, 1)
                        nc.scalar.activation(a_neg[:, :, :], alog[:, :, :], ACT.Exp).then_inc(s_aexp, 1)
                    if g == -1 and s == 0:
                        nc.scalar.preload_act_table_set("silu_and_others")
                    if norm and s == N_STATS[g]:
                        rstd(s_fvar, (f_rs, f_ve), m2 + 1, s_frs)
                    if norm and s == read_step("f", "tr", 0, False):
                        fb2 = m2 // CHUNKS
                        if m2:
                            wait_job(act, "f", "z", 1, m2 - 1)
                        else:
                            act.wait_ge(s_const, 1)
                        if m2 % CHUNKS:
                            nc.scalar.activation(f_hT[:, 0:HALO], f_hT[:, T:T + HALO], ACT.Copy).then_inc(s_halo, 1)
                        else:
                            nc.scalar.activation(f_hT[:, 0:HALO], zeros[:, :], ACT.Copy).then_inc(s_halo, 1)
                        wait_job(act, "f", "tr", 0, m2)
                        if m2 == 0:
                            act.wait_ge(s_wcv, 16 * n_conv)
                            act.wait_ge(s_modc, 1)
                        act.wait_ge(s_halo, m2 + 1)
                        nc.scalar.activation(f_hT[:, HALO:HALO + T], job("f", "tr", 0, m2)[1][:, :], ACT.Identity,
                                             scale=mod_col[:, 1, fb2:fb2 + 1],
                                             bias=mod_col[:, 0, fb2:fb2 + 1]).then_inc(s_read["f", "act"], 1)
                    for half in range(HALVES):
                        if front and s == read_step("f", "xp", half, False):
                            wait_job(act, "f", "xp", half, f)
                            nc.scalar.activation(zu[:, f % 2, HALVES + half, :], job("f", "xp", half, f)[1][:, :],
                                                 ACT.Identity,
                                                 bias=cbias[:, half:half + 1]).then_inc(s_read["f", "act"], 1)
                        if front and s == read_step("f", "z", half, False):
                            wait_job(act, "f", "z", half, f)
                            if f >= 2:
                                act.wait_ge(s_gate, HALVES * (f - 2) + half + 1)
                            nc.scalar.activation(zu[:, f % 2, half, :], job("f", "z", half, f)[1][:, :],
                                                 ACT.Copy).then_inc(s_read["f", "act"], 1)
                    if front and s == (F_SILU if f else F_SILU_0):
                        wait_read(act, "f", "xp", 1, f)
                        u_part = zu[:, f % 2, HALVES:, :]
                        nc.scalar.activation(u_part, u_part, ACT.Silu).then_inc(s_silu, 1)
                        for fz in ((), (0, 1))[f] if f < 2 else (f,):
                            wait_read(act, "f", "z", 1, fz)
                            z_part = zu[:, fz % 2, 0:HALVES, :]
                            nc.scalar.activation(z_part, z_part, ACT.Silu).then_inc(s_zsilu, 1)
                    if leaf and s == U_TANH[late]:
                        wait_read(act, "t", "node", 1, u)
                        nc.scalar.activation(go_r[:, :, :], go_r[:, :, :], ACT.Tanh, scale=0.5).then_inc(s_tanh, 1)
                    back = U_TANH[late] if not front else F_SILU if f else F_SILU_0 + 5
                    if s == back and (front or leaf and u < GROUPS - 1):
                        nc.scalar.preload_act_table_set("natural_log_exp_and_others")
                    if tail and late and s == T_XHAT[late] + 3:
                        nc.scalar.preload_act_table_set("silu_and_others")
                    if leaf and s == U_SIG[late]:
                        act.wait_ge(s_tanh, u + 1)
                        nc.scalar.activation(go_r[:, :, :], go_r[:, :, :], ACT.Identity, scale=0.5,
                                             bias=half_col[:, :]).then_inc(s_sig, 1)
                    if front and s == read_step("f", "xd", 0, False):
                        wait_job(act, "f", "xd", 0, f)
                        if f:
                            act.wait_ge(s_cst, 16 * f)
                        xd_bank = job("f", "xd", 0, f)[1]
                        nc.scalar.activation(xd[:, :], xd_bank[:, :], ACT.Copy).then_inc(s_read["f", "act"], 1)
                    if front and s == F_HI:
                        nc.scalar.activation(b_parts[:, f % 2, :], xd_bank[:, :], ACT.Copy).then_inc(s_hi, 1)
                    if front and s == F_MID:
                        act.wait_ge(s_r1, f + 1)
                        nc.scalar.activation(b_parts[B_MID:P, f % 2, :], xd_bank[B_MID:P, :],
                                             ACT.Copy).then_inc(s_mid, 1)
                    if front and s == F_LO:
                        act.wait_ge(s_r2, f + 1)
                        nc.scalar.activation(b_parts[B_LO:P, f % 2, :], xd_bank[B_LO:P, :],
                                             ACT.Copy).then_inc(s_lo, 1)
                    if front and s in F_ABS:
                        half = F_ABS.index(s)
                        wait_job(act, "f", "dt", half, f)
                        bank = job("f", "dt", half, f)[1]
                        if f:
                            act.wait_ge(s_delta, HALVES * f)
                        nc.scalar.activation(delta[:, f % 2, half, :], bank[:, :], ACT.Relu,
                                             bias=dtb[:, half:half + 1])
                        nc.scalar.activation(sp_abs[:, half, :], bank[:, :], ACT.Abs,
                                             bias=dtb[:, half:half + 1]).then_inc(s_read["f", "act"], 1)
                    if front and s in F_SP:
                        at = F_SP.index(s)
                        if at == 0:
                            wait_read(act, "f", "dt", 1, f)
                        ins, done = softplus_parts(f, at)
                        seq += done is s_aseq
                        ins.then_inc(done, 1)
                    if tail and s == T_RSTD[late]:
                        rstd(s_tvar, (t_rs, t_ve), t + 1, s_trs)
                    for half in range(HALVES):
                        if tail and s == read_step("t", "yt", half, late):
                            wait_job(act, "t", "yt", half, t)
                            nc.scalar.activation(ygT[:, half, :], job("t", "yt", half, t)[1][:, :],
                                                 ACT.Copy).then_inc(s_read["t", "act"], 1)
                    if tail and s == read_step("t", "tr", 0, late):
                        wait_job(act, "t", "tr", 0, t)
                        nc.scalar.activation(t_hT[:, :], job("t", "tr", 0, t)[1][:, :], ACT.Identity,
                                             scale=mod_col[:, 4, tb:tb + 1],
                                             bias=mod_col[:, 3, tb:tb + 1]).then_inc(s_read["t", "act"], 1)
                    for part in range(2):
                        if leaf and s == read_step("t", "pt", part, late):
                            wait_job(act, "t", "pt", part, u)
                            if u and part == 0:
                                wait_job(act, "t", "ff", 0, u - 1)
                            nc.scalar.activation(probT[:, part, :], job("t", "pt", part, u)[1][:, :],
                                                 ACT.Copy).then_inc(s_read["t", "act"], 1)
                        if tail and s == read_step("t", "node", part, late):
                            wait_job(act, "t", "node", part, t)
                            if t:
                                act.wait_ge(s_prob, t)
                            nc.scalar.activation(go_r[:, 2 * part:2 * part + 2, :],
                                                 job("t", "node", part, t)[1][:, :].rearrange(
                                                     "p (i n) -> p i n", n=LEAVES),
                                                 ACT.Copy).then_inc(s_read["t", "act"], 1)

        @block.tensor
        def _(pe):
            def transpose(dst, src):
                return nc.tensor.transpose(dst, src, ident[:, :])

            def keep_warm(count):
                for _ in range(count):
                    nc.tensor.matmul(bb[RB - 1][:, :], idle[:, 0:P], idle[:, :], start=True, stop=True)

            pe.wait_ge(s_idle, 1)
            keep_warm(WARM_START)
            pe.wait_ge(s_const, 1)
            pe.wait_ge(s_wmod, 16 * n_mod)
            pe.wait_ge(s_csilu, 1)
            for m in range(6):
                last = nc.tensor.matmul(yb[0][:, m * BATCH:(m + 1) * BATCH], w_mod[:, m, :], c_silu[:, :],
                                        start=True, stop=True)
            last.then_inc(s_pre_pe, 1)

            def gate_products():
                pe.wait_ge(s_cwide, 1)
                for b in range(BATCH):
                    for i, m in enumerate((2, 5)):
                        last = nc.tensor.matmul(yb[1][:, (2 * b + i) * DM:(2 * b + i + 1) * DM], c_wide[:, b, :],
                                                w_mod[:, m, :], start=True, stop=True)
                last.then_inc(s_pre_pe, 1)

            def dt_weight_transposes():
                pe.wait_ge(s_wfront, 16 * n_front)
                for hh in range(HALVES):
                    last = nc.tensor.transpose(bb[0][0:R, hh * P:(hh + 1) * P], w_dtin[:, hh, :], ident[:, :])
                last.then_inc(s_wdtt, 1)

            def dt_weight_products():
                pe.wait_ge(s_wdtc, 1)
                for hh in range(HALVES):
                    last = nc.tensor.matmul(bb[1][:, hh * DI:(hh + 1) * DI], w_dtin_t[:, hh * P:(hh + 1) * P],
                                            w_dt[:, :], start=True, stop=True)
                last.then_inc(s_wdtp, 1)

            def weight_transposes():
                pe.wait_ge(s_w, 16 * n_rest)
                pe.wait_ge(s_wdt, 1)
                for i in range(2):
                    transpose(bb[0][:, i * P:(i + 1) * P], rout[:, i, :])
                    transpose(bb[1][:, i * P:(i + 1) * P], leafv[:, i, :])
                transpose(bb[2][:, 0:P], wo).then_inc(s_pre_pe, 1)

            def weight_products():
                pe.wait_ge(s_pre_cp, 1)
                nc.tensor.matmul(mb["t"][0][:, 0:2 * P], wq[:, :], rout_t[:, :], start=True, stop=True)
                for i in range(2):
                    last = nc.tensor.matmul(mb["t"][0][:, (2 + i) * DM:(3 + i) * DM],
                                            leafv_t[:, i * P:(i + 1) * P], wo_t[:, :], start=True, stop=True)
                last.then_inc(s_pre_pe, 1)

            def product(g, side, name, part, piece, pieces):
                n, bank = job(side, name, part, g)
                b = g // CHUNKS
                if piece == 0:
                    wait_bank(pe, side, n)
                tiles = range(piece * TILES // pieces, (piece + 1) * TILES // pieces)
                if (side, name) == ("f", "tr"):
                    pe.wait_ge(s_fxh, g + 1)
                    for i in tiles:
                        last = transpose(bank[:, i * P:(i + 1) * P], f_xhat[:, i, :])
                elif name == "xp":
                    if piece == 0:
                        wait_read(pe, "f", "tr", 0, g)
                        if g == 0:
                            pe.wait_ge(s_wconv, 1)
                    for tap in range(piece * TAPS // pieces, (piece + 1) * TAPS // pieces):
                        last = nc.tensor.matmul(bank[:, :], w_conv[:, tap, part * P:(part + 1) * P],
                                                f_hT[:, tap:tap + T], start=tap == 0, stop=tap == TAPS - 1)
                elif name == "z":
                    wait_read(pe, "f", "tr", 0, g)
                    for i in tiles:
                        last = nc.tensor.matmul(bank[:, i * P:(i + 1) * P],
                                                f_hT[:, HALO + i * P:HALO + (i + 1) * P],
                                                w_in[:, DI + part * P:DI + (part + 1) * P], start=True, stop=True)
                elif name == "xd":
                    if piece == 0:
                        pe.wait_ge(s_silu, g + 1)
                    last = nc.tensor.matmul(bank[:, :], w_xp[:, piece, :], zu[:, g % 2, HALVES + piece, :],
                                            start=piece == 0, stop=piece == HALVES - 1)
                elif name == "dt":
                    if piece == 0:
                        pe.wait_ge(s_silu, g + 1)
                        if g == 0:
                            pe.wait_ge(s_wdt, 1)
                    last = nc.tensor.matmul(bank[:, :], w_xdt[:, piece, part * P:(part + 1) * P],
                                            zu[:, g % 2, HALVES + piece, :],
                                            start=piece == 0, stop=piece == HALVES - 1)
                elif name == "yt":
                    pe.wait_ge(s_gate, HALVES * g + part + 1)
                    for i in tiles:
                        last = transpose(bank[:, i * P:(i + 1) * P], yg[:, part, i * P:(i + 1) * P])
                elif name == "out":
                    if piece == 0:
                        wait_read(pe, "t", "yt", 1, g)
                        if g == 0:
                            pe.wait_ge(s_wready, 1)
                    for i in tiles:
                        for hh in range(HALVES):
                            last = nc.tensor.matmul(bank[:, i * P:(i + 1) * P], ygT[:, hh, i * P:(i + 1) * P],
                                                    w_out_g[:, b, hh, :], start=hh == 0, stop=hh == HALVES - 1)
                elif (side, name) == ("t", "tr"):
                    pe.wait_ge(s_txh, g + 1)
                    for i in tiles:
                        last = transpose(bank[:, i * P:(i + 1) * P], t_xhat[:, i, :])
                elif name == "node":
                    wait_read(pe, "t", "tr", 0, g)
                    for i in range(2):
                        tile = 2 * part + i
                        last = nc.tensor.matmul(bank[:, i * LEAVES:(i + 1) * LEAVES],
                                                t_hT[:, tile * P:(tile + 1) * P], w_node[:, :],
                                                start=True, stop=True)
                elif name == "pt":
                    pe.wait_ge(s_prob, g + 1)
                    for i in tiles:
                        last = transpose(bank[:, i * P:(i + 1) * P],
                                         prob[(DEPTH - 1) % 2][:, i, part * P:(part + 1) * P])
                else:
                    if piece == 0:
                        wait_read(pe, "t", "pt", 1, g)
                    for i in tiles:
                        dst = bank[:, i * P:(i + 1) * P]
                        nc.tensor.matmul(dst, ones[0:1, :], wo_b_g[0:1, b, :], start=True, stop=False)
                        for hh in range(2):
                            last = nc.tensor.matmul(dst, probT[:, hh, i * P:(i + 1) * P], leaf_out_g[:, b, hh, :],
                                                    start=False, stop=hh == 1)
                if piece == pieces - 1:
                    last.then_inc(s_job[side], 1)

            for g in range(FIRST, LAST + 1):
                f = g + 1
                front = 0 <= f < GROUPS
                for s in range(STEPS):
                    k = g * STEPS + s
                    kf, ks = k + AHEAD_FILL, k - LAG_SUM
                    if 0 <= kf < K and kf % HALVES == 0:
                        pair = kf // HALVES
                        gf, n = divmod(pair, N)
                        if n == 0:
                            pe.wait_ge(s_lo, gf + 1)
                        if pair == 0:
                            pe.wait_ge(s_pre_cp, 1)
                        if pair >= RB:
                            pe.wait_ge(s_dbu, pair - RB + 1)
                        nc.tensor.matmul(bb[pair % RB][:, :], sel[:, n, :], b_parts[:, gf % 2, :],
                                         start=True, stop=True).then_inc(s_fill, 1)
                    if 0 <= ks < K:
                        gs, ss = divmod(ks, STEPS)
                        n, half = divmod(ss, HALVES)
                        hg = HALVES * gs + half
                        bank = yb[hg % RY]
                        tiles = [slice(i * P, (i + 1) * P) for i in range(TILES)]
                        if n == 0:
                            if hg >= RY:
                                pe.wait_ge(s_gate, hg - RY + 1)
                            for tile in tiles:
                                nc.tensor.matmul(bank[:, tile], zu[:, gs % 2, HALVES + half, tile],
                                                 diag_d[:, half, :], start=tile.start == 0, stop=False,
                                                 skip_group_check=True)
                        pe.wait_ge(s_hc, ks // HALVES + 1)
                        for tile in tiles:
                            last = nc.tensor.matmul(bank[:, tile], h[:, ks // HALVES % RP, half, tile], ident[:, :],
                                                    start=False, stop=n == N - 1, is_transpose=True,
                                                    skip_group_check=True)
                        last.then_inc(s_sum, 1)
                    for side in JOBS:
                        for (name, part), (off, *by_phase) in JOBS[side].items():
                            steps = by_phase[g >= GROUPS]
                            if s in steps and 0 <= g + off < GROUPS:
                                product(g + off, side, name, part, steps.index(s), len(steps))
                    if front and s in (F_R1, F_R2):
                        if s == F_R1:
                            pe.wait_ge(s_const, 2)
                            wait_read(pe, "f", "xd", 0, f)
                            pe.wait_ge(s_hi, f + 1)
                        else:
                            pe.wait_ge(s_mid, f + 1)
                        nc.tensor.matmul(job("f", "xd", 0, f)[1][:, :], neg_ident[:, :], b_parts[:, f % 2, :],
                                         start=False, stop=True,
                                         skip_group_check=True).then_inc(s_r1 if s == F_R1 else s_r2, 1)
                    if g == FIRST and s == 29:
                        dt_weight_transposes()
                    if g == -1 and s == 1:
                        dt_weight_products()
                    if g == -1 and s == 5:
                        gate_products()
                    if g == -1 and s == 16:
                        weight_transposes()
                    if g == -1 and s == 17:
                        weight_products()
                    if (g, s) in WARM:
                        if g >= GROUPS:
                            pe.wait_ge(s_dbu, PAIRS)
                        keep_warm(WARM[g, s])

        @block.vector
        def _(dve):
            seq = 0

            def chain(ins):
                nonlocal seq
                seq += 1
                ins.then_inc(s_dseq, 1)
                dve.wait_ge(s_dseq, seq)

            v = nc.vector

            def stats(g, bn, mv, ve, ready):
                for i in range(TILES):
                    last = v.bn_stats(bn[:, i, :], xs[:, g * TILES + i, :])
                chain(last)
                for i in range(TILES):
                    last = v.bn_aggr(mv[:, i, :], bn[:, i, :])
                chain(last)
                v.tensor_scalar(ve[:, :], mv[:, :, 1], EPS, None, ALU.add).then_inc(ready, 1)

            def normalise(g, mv, rs, rs_ready, xhat, ready):
                dve.wait_ge(rs_ready, g + 1)
                for i in range(TILES):
                    last = v.tensor_scalar(xhat[:, i, :], xs[:, g * TILES + i, :], mv[:, i, 0:1], rs[:, i:i + 1],
                                           ALU.subtract, ALU.mult)
                last.then_inc(ready, 1)

            def front_weights():
                dve.wait_ge(s_csilu, 1)
                dve.wait_ge(s_const, 1)
                for b in range(BATCH):
                    last = v.tensor_scalar(c_wide[:, b, :], ones[:, :], c_silu[:, b:b + 1], None, ALU.mult)
                last.then_inc(s_cwide, 1)
                dve.wait_ge(s_pre_pe, 1)
                chain(v.tensor_copy(mod_col[:, :, :], yb[0][:, 0:6 * BATCH].rearrange("p (m b) -> p m b", b=BATCH)))
                v.tensor_scalar(mod_col[:, 1, :], mod_col[:, 1, :], 1.0, None, ALU.add)
                v.tensor_scalar(mod_col[:, 4, :], mod_col[:, 4, :], 1.0, None, ALU.add).then_inc(s_modc, 1)
                dve.wait_ge(s_wcv, 16 * n_conv)
                for tap in range(TAPS):
                    last = v.tensor_tensor(w_conv[:, tap, :], w_in[:, 0:DI], taps[:, :, tap], ALU.mult)
                last.then_inc(s_wconv, 1)
                dve.wait_ge(s_wdtt, 1)
                v.tensor_copy(w_dtin_t[:, :], bb[0][0:R, 0:DI]).then_inc(s_wdtc, 1)

                dve.wait_ge(s_wdtp, 1)
                v.tensor_copy(w_xdt[:, :, :],
                              bb[1][:, 0:HALVES * DI].rearrange("p (h e) -> p h e", h=HALVES)).then_inc(s_wdt, 1)

            def gates():
                dve.wait_ge(s_pre_pe, 2)
                chain(v.tensor_copy(gate_raw[:, :, :, :],
                                    yb[1][:, :].rearrange("p (b i d) -> p b i d", b=BATCH, i=2)))
                v.tensor_scalar(gate_sgn[:, :, :, :], gate_raw[:, :, :, :], 0.0, 2.0, ALU.is_ge, ALU.mult)
                chain(v.scalar_tensor_tensor(gate_abs[:, :, :, :], gate_raw[:, :, :, :], -1.0,
                                             gate_raw[:, :, :, :], ALU.mult, ALU.max))
                chain(v.tensor_scalar(gate_abs[:, :, :, :], gate_abs[:, :, :, :], GATE_MIN, None, ALU.max))
                chain(v.scalar_tensor_tensor(gate_raw[:, :, :, :], gate_sgn[:, :, :, :], -1.0,
                                             gate_abs[:, :, :, :], ALU.add, ALU.mult))

            def scan_weights():
                dve.wait_ge(s_w, 16 * n_rest)
                for hh in range(HALVES):
                    v.tensor_scalar(diag_d[:, hh, :], ident[:, :], dskip[:, hh:hh + 1], None, ALU.mult)
                dve.wait_ge(s_aexp, 1)
                v.tensor_scalar(a_neg[:, :, :], a_neg[:, :, :], -1.0, None, ALU.mult).then_inc(s_aneg, 1)
                dve.wait_ge(s_pre_pe, 3)
                v.tensor_copy(rout_t[:, :], bb[0][:, 0:2 * P])
                v.tensor_copy(wo_t[:, :], bb[2][:, 0:P])
                v.tensor_copy(leafv_t[:, :], bb[1][:, 0:2 * P]).then_inc(s_pre_cp, 1)

            def tail_weights():
                dve.wait_ge(s_pre_pe, 4)
                v.tensor_copy(w_node[:, :], mb["t"][0][:, 0:2 * P])
                chain(v.tensor_copy(leaf_out[:, :, :],
                                    mb["t"][0][:, 2 * DM:4 * DM].rearrange("p (i d) -> p i d", d=DM)))
                for b in range(BATCH):
                    for i in range(2):
                        v.tensor_tensor(w_out_g[:, b, i, :], w_out[:, i, :], gate_raw[:, b, 0, :], ALU.mult)
                        v.tensor_tensor(leaf_out_g[:, b, i, :], leaf_out[:, i, :], gate_raw[:, b, 1, :], ALU.mult)
                    last = v.tensor_tensor(wo_b_g[0:1, b, :], wo_b[0:1, :], gate_raw[0:1, b, 1, :], ALU.mult)
                last.then_inc(s_wready, 1)

            for g in range(FIRST, LAST + 1):
                m2, f, t, u, late = g + 2, g + 1, g - 1, g - 2, g >= GROUPS
                norm, front, tail, leaf = m2 < GROUPS, 0 <= f < GROUPS, 0 <= t < GROUPS, 0 <= u < GROUPS
                for s in range(STEPS):
                    if g == FIRST and s == N_XHAT[g] + 1:
                        front_weights()
                    if g == -1 and s == 8:
                        gates()
                    if g == -1 and s == 16:
                        scan_weights()
                    if g == -1 and s == F_DELTA + 1:
                        tail_weights()
                    k = g * STEPS + s
                    if 0 <= k < K:
                        n, half = divmod(s, HALVES)
                        pair = k // HALVES
                        dve.wait_ge(s_dA, k + 1)
                        if half == 0:
                            dve.wait_ge(s_dbu, pair + 1)
                            if pair >= RP:
                                dve.wait_ge(s_sum, HALVES * (pair - RP + 1))
                            if g % CHUNKS:
                                dve.wait_ge(s_save, saves(pair - N) + 1)
                        start = state[:, n, half:half + 1] if g % CHUNKS else 0.0
                        v.tensor_tensor_scan(h[:, pair % RP, half, :], dA[:, k % RD, :], dbu[:, pair % RW, half, :],
                                             start, ALU.mult, ALU.add).then_inc(s_scan, 1)
                        if half == 0 and pair and saved(pair - 1):
                            dve.wait_ge(s_scan, k)
                            v.tensor_copy(state[:, (pair - 1) % N, :],
                                          h[:, (pair - 1) % RP, :, T - 1]).then_inc(s_save, 1)
                    kd = k + AHEAD_DBU
                    if 0 <= kd < K and kd % HALVES == 0:
                        pair = kd // HALVES
                        gd, n = divmod(pair, N)
                        if n == 0:
                            dve.wait_ge(s_du, HALVES * (gd + 1))
                        dve.wait_ge(s_fill, pair + 1)
                        if pair >= RW:
                            dve.wait_ge(s_scan, HALVES * (pair - RW + 1))
                        v.tensor_tensor(dbu[:, pair % RW, :, :], du[:, gd % 2, :, :],
                                        bb[pair % RB][:, :].unsqueeze(1).broadcast_to([P, HALVES, T]),
                                        ALU.mult).then_inc(s_dbu, 1)
                    if norm and s == N_STATS[g]:
                        if m2 == 0:
                            dve.wait_ge(s_x0, 16)
                        else:
                            dve.wait_ge(s_x, 16 * (GROUPS - 1))
                        stats(m2, f_bn, f_mv, f_ve, s_fvar)
                    if norm and s == N_XHAT[g]:
                        if m2:
                            wait_job(dve, "f", "tr", 0, m2 - 1)
                        normalise(m2, f_mv, f_rs, s_frs, f_xhat, s_fxh)
                    if front and s in F_POLY:
                        at = F_POLY.index(s)
                        if at == 0:
                            dve.wait_ge(s_poly, f + 1)
                        else:
                            dve.wait_ge(s_dseq, poly_seq)
                        if at < 2:
                            last = v.scalar_tensor_tensor(sp_t[:, :, :], sp_t[:, :, :], (7.0 / 18.0, -1.0)[at],
                                                          sp_e[:, :, :], ALU.add, ALU.mult)
                        else:
                            dve.wait_ge(s_sp, f + 1)
                            last = v.scalar_tensor_tensor(sp_ln[:, :, :], sp_t[:, :, :], -LOG_KNEE,
                                                          sp_ln[:, :, :], ALU.max, ALU.subtract)
                        seq += 1
                        last.then_inc(s_dseq, 1)
                        poly_seq = seq
                    if front and s == F_DELTA:
                        dve.wait_ge(s_dseq, poly_seq)
                        for half in range(HALVES):
                            v.tensor_tensor(delta[:, f % 2, half, :], delta[:, f % 2, half, :], sp_ln[:, half, :],
                                            ALU.subtract).then_inc(s_delta, 1)
                    if tail and s in T_GATE[late]:
                        half = T_GATE[late].index(s)
                        hg = HALVES * t + half
                        dve.wait_ge(s_sum, t * STEPS + STEPS - HALVES + half + 1)
                        dve.wait_ge(s_zsilu, t + 1)
                        if t:
                            wait_job(dve, "t", "yt", half, t - 1)
                        v.tensor_tensor(yg[:, half, :], yb[hg % RY][:, :], zu[:, t % 2, half, :],
                                        ALU.mult).then_inc(s_gate, 1)
                    if tail and s == T_ADD[late]:
                        wait_job(dve, "t", "out", 0, t)
                        x1 = xs[:, t * TILES:(t + 1) * TILES, :]
                        v.tensor_tensor(x1, job("t", "out", 0, t)[1][:, :].rearrange("p (i d) -> p i d", d=DM), x1,
                                        ALU.add).then_inc(s_read["t", "dve"], 1)
                    if tail and s == T_STATS[late]:
                        wait_read(dve, "t", "out", 0, t)
                        stats(t, t_bn, t_mv, t_ve, s_tvar)
                    if tail and s == T_XHAT[late]:
                        if t:
                            wait_job(dve, "t", "tr", 0, t - 1)
                        normalise(t, t_mv, t_rs, s_trs, t_xhat, s_txh)
                    if u == GROUPS - 1 and s == U_LEAF[late][0]:
                        dve.wait_ge(s_sig, u + 1)
                        wait_job(dve, "t", "pt", 1, u - 1)
                        for level in range(DEPTH):
                            chain(leaf_products(v, level, 1))
                            last = leaf_products(v, level, 0)
                            if level < DEPTH - 1:
                                chain(last)
                        last.then_inc(s_prob, 1)
                    if leaf and s == U_FIN[late]:
                        wait_job(dve, "t", "ff", 0, u)
                        x1 = xs[:, u * TILES:(u + 1) * TILES, :]
                        v.tensor_tensor(x1, job("t", "ff", 0, u)[1][:, :].rearrange("p (i d) -> p i d", d=DM), x1,
                                        ALU.add).then_inc(s_read["t", "dve"], 1)


_INS = ["L0_attn_x", "L0_attn_W_in", "L0_attn_conv_w", "L0_attn_conv_b", "L0_attn_W_xp", "L0_attn_W_dt",
        "L0_attn_dt_bias", "L0_attn_A_log", "L0_attn_D_skip", "L0_attn_W_out", "L0_ffn_Wq", "L0_ffn_routers",
        "L0_ffn_leaf_values", "L0_ffn_Wout_w", "L0_ffn_Wout_b", "L0_c", "L0_wmod"]
_OUTS = [((2, 2048, 128), "float32")]


def kernel(**inputs):
    import numpy as _np
    import concourse.bacc as _bacc
    from concourse import mybir as _mybir
    from concourse.bass_utils import run_bass_kernel_spmd as _run

    nc = _bacc.Bacc("TRN2", target_bir_lowering=False, num_devices=1)
    arrays, args = {}, []
    for name in _INS:
        a = _np.ascontiguousarray(inputs[name])
        arrays[f"in_{name}_dram"] = a
        args.append(nc.dram_tensor(f"in_{name}_dram", a.shape, _mybir.dt.from_np(a.dtype), kind="ExternalInput").ap())
    for i, (shape, dtype) in enumerate(_OUTS):
        dt = _mybir.dt.from_np(_np.dtype(dtype))
        args.append(nc.dram_tensor(f"out_{i}_dram", shape, dt, kind="ExternalOutput").ap())
    bass_adaln_mamba_tree_ffn_kernel(nc, *args)
    r = _run(nc, [arrays], core_ids=[0])
    got = tuple(r.results[0][f"out_{i}_dram"] for i in range(len(_OUTS)))
    return got[0]
```
